# Optimizing a Trainium2 kernel written in Bass

```python
import numpy as np
import jax
import jax.numpy as jnp

def _softmax(x, axis=-1):
    return jax.nn.softmax(x, axis=axis)

def _gelu(x):
    return jax.nn.gelu(x, approximate=True)

def _silu(x):
    return jax.nn.silu(x)

def _sigmoid(x):
    return jax.nn.sigmoid(x)

def _layernorm(x, axis=-1, eps=1e-05):
    m = jnp.mean(x, axis=axis, keepdims=True)
    v = jnp.var(x, axis=axis, keepdims=True)
    return (x - m) / jnp.sqrt(v + eps)

def _scatter_add(tgt, idx, src, axis=0):
    return tgt.at[idx].add(src)

def _segment_sum(src, seg, n):
    return jax.ops.segment_sum(src, seg, n)
kernel_name = 'mk_sandwich_d1_jaxref_r8_bec695'

def setup_inputs(seed: int=0):
    np.random.seed(seed)
    _w = jnp.asarray

    def _L0_attn_setup():
        import jax, jax.numpy as jnp
        import numpy as np
        B, N, E, H = (2, 256, 128, 16)
        D = E // H
        EPS = 1e-05
        SCALE = D ** (-0.5)
        STD = 0.02
        key = jax.random.key(seed)
        ks = jax.random.split(key, 10)
        rn = lambda k, shape: jax.random.normal(k, shape, dtype=jnp.float32)
        x = rn(ks[0], (B, N, E))
        Wq = rn(ks[1], (E, E)) * STD
        Wk = rn(ks[2], (E, E)) * STD
        Wv = rn(ks[3], (E, E)) * STD
        Wo = rn(ks[4], (E, E)) * STD
        Wf1 = rn(ks[5], (E, D)) * STD
        Wf2 = rn(ks[6], (D, E)) * STD
        Wg1 = rn(ks[7], (E, D)) * STD
        Wg2 = rn(ks[8], (D, E)) * STD
        norm_weight = jnp.ones((E,), dtype=jnp.float32)
        return dict(x=x, Wq=Wq, Wk=Wk, Wv=Wv, Wo=Wo, Wf1=Wf1, Wf2=Wf2, Wg1=Wg1, Wg2=Wg2, norm_weight=norm_weight)
    _L0_attn_in = _L0_attn_setup()

    def _L0_ffn_setup():
        import jax, jax.numpy as jnp
        import numpy as np
        H = 128
        D = 344
        E = 8
        TOP_K = 2

        def _moe_ffn(x, gate_w, we_gate, we_up, we_down, sw_gate, sw_up, sw_down):
            B, S, h = x.shape
            xt = x.reshape(-1, h)
            T = xt.shape[0]
            logits = xt @ gate_w.T
            probs = jax.nn.softmax(logits, axis=-1)
            topk_w, topk_idx = jax.lax.top_k(probs, TOP_K)
            topk_w = topk_w / (jnp.sum(topk_w, axis=-1, keepdims=True) + 1e-20)
            cw = jnp.zeros((T, E), dtype=xt.dtype).at[jnp.arange(T)[:, None], topk_idx].add(topk_w)
            g = jnp.einsum('th,ehd->etd', xt, we_gate)
            u = jnp.einsum('th,ehd->etd', xt, we_up)
            hidden = jax.nn.silu(g) * u
            eo = jnp.einsum('etd,edh->eth', hidden, we_down)
            y = jnp.einsum('te,eth->th', cw, eo)
            y = y + jax.nn.silu(xt @ sw_gate) * (xt @ sw_up) @ sw_down
            return y.reshape(B, S, h)
        key = jax.random.key(seed)
        ks = jax.random.split(key, 8)
        s = 0.02
        return {'x': jax.random.normal(ks[0], (2, 256, H), dtype=jnp.float32), 'gate_w': jax.random.normal(ks[1], (E, H), dtype=jnp.float32) * s, 'we_gate': jax.random.normal(ks[2], (E, H, D), dtype=jnp.float32) * s, 'we_up': jax.random.normal(ks[3], (E, H, D), dtype=jnp.float32) * s, 'we_down': jax.random.normal(ks[4], (E, D, H), dtype=jnp.float32) * s, 'sw_gate': jax.random.normal(ks[5], (H, D), dtype=jnp.float32) * s, 'sw_up': jax.random.normal(ks[6], (H, D), dtype=jnp.float32) * s, 'sw_down': jax.random.normal(ks[7], (D, H), dtype=jnp.float32) * s}
    _L0_ffn_in = _L0_ffn_setup()
    _d = {'L0_attn_x': _L0_attn_in['x'], 'L0_attn_Wq': _L0_attn_in['Wq'], 'L0_attn_Wk': _L0_attn_in['Wk'], 'L0_attn_Wv': _L0_attn_in['Wv'], 'L0_attn_Wo': _L0_attn_in['Wo'], 'L0_attn_Wf1': _L0_attn_in['Wf1'], 'L0_attn_Wf2': _L0_attn_in['Wf2'], 'L0_attn_Wg1': _L0_attn_in['Wg1'], 'L0_attn_Wg2': _L0_attn_in['Wg2'], 'L0_attn_norm_weight': _L0_attn_in['norm_weight'], 'L0_ffn_gate_w': _L0_ffn_in['gate_w'], 'L0_ffn_we_gate': _L0_ffn_in['we_gate'], 'L0_ffn_we_up': _L0_ffn_in['we_up'], 'L0_ffn_we_down': _L0_ffn_in['we_down'], 'L0_ffn_sw_gate': _L0_ffn_in['sw_gate'], 'L0_ffn_sw_up': _L0_ffn_in['sw_up'], 'L0_ffn_sw_down': _L0_ffn_in['sw_down']}
    _x0 = _d['L0_attn_x']
    _d['L0_attn_x'] = jax.random.normal(jax.random.fold_in(jax.random.key(seed), 1), (1, 2048, 128), dtype=_x0.dtype)
    del _x0
    return _d

def reference(L0_attn_x, L0_attn_Wq, L0_attn_Wk, L0_attn_Wv, L0_attn_Wo, L0_attn_Wf1, L0_attn_Wf2, L0_attn_Wg1, L0_attn_Wg2, L0_attn_norm_weight, L0_ffn_gate_w, L0_ffn_we_gate, L0_ffn_we_up, L0_ffn_we_down, L0_ffn_sw_gate, L0_ffn_sw_up, L0_ffn_sw_down):

    def _L0_attn_ref(x, Wq, Wk, Wv, Wo, Wf1, Wf2, Wg1, Wg2, norm_weight):
        import jax, jax.numpy as jnp
        import numpy as np
        B, N, E, H = (2, 256, 128, 16)
        D = E // H
        EPS = 1e-05
        SCALE = D ** (-0.5)
        STD = 0.02
        b, n, e = x.shape
        q = jax.nn.silu(x @ Wq).reshape(b, n, H, D)
        k = jax.nn.silu(x @ Wk).reshape(b, n, H, D)
        v = (x @ Wv).reshape(b, n, H, D)
        f = jax.nn.sigmoid(x @ Wf1 @ Wf2).reshape(b, n, H, D)

        def step(S, qkvf):
            qt, kt, vt, ft = qkvf
            S = ft[..., :, None] * S + kt[..., :, None] * vt[..., None, :]
            ot = jnp.einsum('bhk,bhkv->bhv', qt, S)
            return (S, ot)
        S0 = jnp.zeros((b, H, D, D), x.dtype)
        xs = (jnp.moveaxis(q, 1, 0) * SCALE, jnp.moveaxis(k, 1, 0), jnp.moveaxis(v, 1, 0), jnp.moveaxis(f, 1, 0))
        _, o = jax.lax.scan(step, S0, xs)
        o = jnp.moveaxis(o, 0, 1).reshape(b, n, e)
        g = jax.nn.sigmoid(x @ Wg1 @ Wg2)
        og = (o * g).reshape(b, n, H, D)
        og = og * jax.lax.rsqrt(jnp.mean(og * og, axis=-1, keepdims=True) + EPS)
        o = og.reshape(b, n, e) * norm_weight
        return o @ Wo

    def _L0_ffn_ref(x, gate_w, we_gate, we_up, we_down, sw_gate, sw_up, sw_down):
        import jax, jax.numpy as jnp
        import numpy as np
        H = 128
        D = 344
        E = 8
        TOP_K = 2

        def _moe_ffn(x, gate_w, we_gate, we_up, we_down, sw_gate, sw_up, sw_down):
            B, S, h = x.shape
            xt = x.reshape(-1, h)
            T = xt.shape[0]
            logits = xt @ gate_w.T
            probs = jax.nn.softmax(logits, axis=-1)
            topk_w, topk_idx = jax.lax.top_k(probs, TOP_K)
            topk_w = topk_w / (jnp.sum(topk_w, axis=-1, keepdims=True) + 1e-20)
            cw = jnp.zeros((T, E), dtype=xt.dtype).at[jnp.arange(T)[:, None], topk_idx].add(topk_w)
            g = jnp.einsum('th,ehd->etd', xt, we_gate)
            u = jnp.einsum('th,ehd->etd', xt, we_up)
            hidden = jax.nn.silu(g) * u
            eo = jnp.einsum('etd,edh->eth', hidden, we_down)
            y = jnp.einsum('te,eth->th', cw, eo)
            y = y + jax.nn.silu(xt @ sw_gate) * (xt @ sw_up) @ sw_down
            return y.reshape(B, S, h)
        return _moe_ffn(x, gate_w, we_gate, we_up, we_down, sw_gate, sw_up, sw_down)
    x = L0_attn_x
    x = x + _layernorm(_L0_attn_ref(_layernorm(x, axis=-1), L0_attn_Wq, L0_attn_Wk, L0_attn_Wv, L0_attn_Wo, L0_attn_Wf1, L0_attn_Wf2, L0_attn_Wg1, L0_attn_Wg2, L0_attn_norm_weight), axis=-1)
    x = x + _layernorm(_L0_ffn_ref(_layernorm(x, axis=-1), L0_ffn_gate_w, L0_ffn_we_gate, L0_ffn_we_up, L0_ffn_we_down, L0_ffn_sw_gate, L0_ffn_sw_up, L0_ffn_sw_down), axis=-1)
    return x

_drawn_inputs = setup_inputs


def setup_inputs(seed=0):
    import zlib

    import numpy as np

    out = dict(_drawn_inputs(seed))
    spreads = {'L0_attn_norm_weight': (1.0, 0.2)}
    factors = {'L0_attn_Wf1': 4.241, 'L0_attn_Wf2': 4.721, 'L0_attn_Wg1': 3.453, 'L0_attn_Wg2': 3.561}
    for name, (base, spread) in spreads.items():
        noise = np.random.default_rng([zlib.crc32(name.encode()), seed]).standard_normal(out[name].shape)
        drawn = base * np.exp(spread * noise) if base else spread * noise
        out[name] = jnp.asarray(drawn.astype(out[name].dtype))
    for name, factor in factors.items():
        out[name] = (out[name] * factor).astype(out[name].dtype)
    return out
```

```python
from contextlib import ExitStack

import concourse.bass as bass
from concourse import mybir

P = 128
F32 = mybir.dt.float32
F32R = mybir.dt.float32r
I32 = mybir.dt.int32
ALU = mybir.AluOpType
ACT = mybir.ActivationFunctionType
AX_X = mybir.AxisListType.X

CHUNK = 512
TILES = CHUNK // P
EPS = 1e-5
RSQRT_MAGIC = 0x5F3759DF
NEWTON_STEPS = 3


def build(nc, x, Wq, Wk, Wv, Wo, Wf1, Wf2, Wg1, Wg2, norm_weight, gate_w,
          we_gate, we_up, we_down, sw_gate, sw_up, sw_down, out):
    _, TOKENS, E = x.shape
    D = Wf1.shape[1]
    HEADS = E // D
    NE, _, FD = we_gate.shape
    NX = NE + 1
    CHUNKS = TOKENS // CHUNK
    SCALE = float(D) ** -0.5
    ROWS = [(j, min(P, FD - j)) for j in range(0, FD, P)]
    NJ = len(ROWS)
    STEPS = NX * NJ
    LO = 32
    STAGE = 2
    assert E == P and TOKENS % CHUNK == 0 and STEPS % 3 == 0 and NE % 2 == 0

    with ExitStack() as ctx:
        def sb(name, shape, dt=F32):
            return ctx.enter_context(nc.sbuf_tensor(name, shape, dt))

        def bank(name):
            return ctx.enter_context(nc.psum_tensor(name, [P, CHUNK], F32))

        def sem(name):
            return ctx.enter_context(nc.semaphore(name))

        w_out = sb("w_out", [P, E])
        raw_fg1 = sb("raw_fg1", [P, 2, D])
        raw_fg2 = sb("raw_fg2", [D, 2, E])
        raw_route = sb("raw_route", [NE, E])
        norm_w = sb("norm_w", [P, 1])
        raw_gu = sb("raw_gu", [P, STAGE, 2, FD])
        raw_down = sb("raw_down", [P, STAGE, NJ, E])
        proj_hi = sb("proj_hi", [P, 4, E], F32R)
        proj_lo = sb("proj_lo", [P, 4, E], F32R)
        vrep_hi = sb("vrep_hi", [P, D, E], F32R)
        vrep_lo = sb("vrep_lo", [P, D, E], F32R)
        fg1_t = sb("fg1_t", [D, 2, E])
        route_t = sb("route_t", [P, NE])
        gu_hi = sb("gu_hi", [P, NX, 2, FD], F32R)
        gu_lo = sb("gu_lo", [P, NX, 2, FD], F32R)
        down_hi = sb("down_hi", [P, NX, NJ, E], F32R)
        down_lo = sb("down_lo", [P, NX, NJ, E], F32R)
        ident = sb("ident", [P, P])
        head_of = sb("head_of", [P, HEADS])
        head_rows = sb("head_rows", [HEADS, P])
        pick_v = sb("pick_v", [P, D, E], F32R)
        pick_expert = sb("pick_expert", [LO + NE, NE, P], F32R)
        order = sb("order", [P, TILES, NE])
        x_res = sb("x_res", [P, TOKENS // P, E])
        stats = sb("stats", [P, TILES, 6])
        moments = sb("moments", [P, TILES, 2])
        var_eps = sb("var_eps", [P, TILES * HEADS])
        minus_half = sb("minus_half", [P, TILES * HEADS])
        rs = sb("rs", [P, TILES * HEADS])
        newton = sb("newton", [P, TILES * HEADS])
        xn = sb("xn", [P, TILES, E])
        xn_hi = sb("xn_hi", [P, CHUNK], F32R)
        xn_lo = sb("xn_lo", [P, CHUNK], F32R)
        q = sb("q", [P, CHUNK])
        k = sb("k", [P, CHUNK])
        f = sb("f", [P, CHUNK])
        g = sb("g", [P, CHUNK])
        state = sb("state", [P, 2, CHUNK])
        carry = sb("carry", [P, D])
        qs = sb("qs", [P, 2, CHUNK])
        qs_hi = sb("qs_hi", [P, 2, CHUNK], F32R)
        qs_lo = sb("qs_lo", [P, 2, CHUNK], F32R)
        og = sb("og", [P, CHUNK])
        rs_rows = sb("rs_rows", [HEADS, CHUNK])
        turns = sb("turns", [P, CHUNK])
        z = sb("z", [P, TILES, NE])
        ez = sb("ez", [P, TILES, NE])
        prob = sb("prob", [P, TILES, NE])
        rest = sb("rest", [P, TILES, NE])
        cand = sb("cand", [P, TILES, NE])
        first = sb("first", [P, TILES, NE])
        second = sb("second", [P, TILES, NE])
        cw = sb("cw", [P, TILES, NE])
        top = sb("top", [P, 8, TILES])
        cw_rows = sb("cw_rows", [LO + NE, 2 * CHUNK], F32R)
        ff = sb("ff", [P, 2 * CHUNK])
        ff_hi = sb("ff_hi", [P, 2 * CHUNK], F32R)
        ff_lo = sb("ff_lo", [P, 2 * CHUNK], F32R)
        xs = sb("xs", [P, 2, CHUNK])
        xs_hi = sb("xs_hi", [P, 2, CHUNK], F32R)
        xs_lo = sb("xs_lo", [P, 2, CHUNK], F32R)
        sg = sb("sg", [P, 2, CHUNK])
        h = sb("h", [P, 2, CHUNK])
        h_hi = sb("h_hi", [P, 3, CHUNK], F32R)
        h_lo = sb("h_lo", [P, 3, CHUNK], F32R)
        y_t = sb("y_t", [P, CHUNK])
        y_stats = sb("y_stats", [P, TILES, 6])
        y_mom = sb("y_mom", [P, TILES, 2])
        x_out = sb("x_out", [P, TILES, E])

        raw_qkv = y_t[:, 0:3 * E].rearrange("p (w e) -> p w e", w=3)
        pick_expert_f = xs[0:LO + NE].rearrange("p a b -> p (a b)").rearrange("p (e m) -> p e m", e=NE)

        gate_ps = [bank("gate_ps0"), bank("gate_ps1")]
        up_ps = [bank("up_ps0"), bank("up_ps1")]
        y_ps = bank("y_ps")
        w_ps = bank("w_ps")
        a_ps = bank("a_ps")
        o_ps = bank("o_ps")
        a_tok = a_ps[:].rearrange("p (i e) -> p i e", e=E)
        w_tok = w_ps[:].rearrange("p (i e) -> p i e", e=E)

        x_in_landed = [sem(f"x_in_landed{c}") for c in range(CHUNKS)]
        attn_w_landed = sem("attn_w_landed")
        small_w_landed = sem("small_w_landed")
        expert_landed = [sem(f"expert_landed{e}") for e in range(NX)]
        out_stored = sem("out_stored")
        pool_const = sem("pool_const")
        consts_made = sem("consts_made")
        stage_cleared = sem("stage_cleared")
        cw_cleared = sem("cw_cleared")
        picks_made = sem("picks_made")
        small_turned = sem("small_turned")
        small_copied = sem("small_copied")
        fg_composed = sem("fg_composed")
        attn_w_hi = sem("attn_w_hi")
        attn_w_ready = sem("attn_w_ready")
        pick_copied = sem("pick_copied")
        expert_hi = sem("expert_hi")
        expert_lo = sem("expert_lo")
        xn_made = sem("xn_made")
        xn_turned = sem("xn_turned")
        xn_hi_made = sem("xn_hi_made")
        xn_lo_made = sem("xn_lo_made")
        qk_projected = sem("qk_projected")
        qk_made = sem("qk_made")
        fg_projected = sem("fg_projected")
        fg_made = sem("fg_made")
        og_made = sem("og_made")
        sq_made = sem("sq_made")
        sq_summed = sem("sq_summed")
        rs_made = sem("rs_made")
        rs_turned = sem("rs_turned")
        rs_copied = sem("rs_copied")
        rs_spread = sem("rs_spread")
        on_made = sem("on_made")
        attn_projected = sem("attn_projected")
        attn_read = sem("attn_read")
        x2n_made = sem("x2n_made")
        x2_turned = sem("x2_turned")
        x2_copied = sem("x2_copied")
        x2_lo_made = sem("x2_lo_made")
        logits_made = sem("logits_made")
        z_made = sem("z_made")
        exp_made = sem("exp_made")
        cw_made = sem("cw_made")
        cw_turned = sem("cw_turned")
        cw_hi_made = sem("cw_hi_made")
        cw_lo_made = sem("cw_lo_made")
        v_spread = sem("v_spread")
        kv_made = sem("kv_made")
        scanned = sem("scanned")
        carried = sem("carried")
        qs_made = sem("qs_made")
        qs_hi_made = sem("qs_hi_made")
        qs_lo_made = sem("qs_lo_made")
        qs_summed = sem("qs_summed")
        cw_spread = sem("cw_spread")
        xs_made = sem("xs_made")
        xs_hi_made = sem("xs_hi_made")
        xs_lo_made = sem("xs_lo_made")
        gate_done = sem("gate_done")
        up_done = sem("up_done")
        silu_done = sem("silu_done")
        h_made = sem("h_made")
        h_hi_made = sem("h_hi_made")
        h_lo_made = sem("h_lo_made")
        down_done = sem("down_done")
        y_copied = sem("y_copied")
        y_turned = sem("y_turned")
        y_read = sem("y_read")
        x_out_made = sem("x_out_made")
        attn_chain = sem("attn_chain")
        y_chain = sem("y_chain")

        def atleast(eng, s, value):
            if not (isinstance(value, int) and value <= 0):
                eng.wait_ge(s, value)

        def cols(c):
            return bass.ds(c * CHUNK, CHUNK)

        def ff_cols(c):
            return bass.ds((c % 2) * CHUNK, CHUNK)

        def tile_of(buf, c, i):
            return buf[:, bass.ds(c * TILES + i, 1), :].squeeze(1)

        def tiles(c):
            return bass.ds(c * TILES, TILES)

        def three(out_ap, w_hi, w_lo, v_hi, v_lo, start=True, stop=True):
            nc.tensor.matmul(out_ap, w_hi, v_hi, start=start, stop=False)
            nc.tensor.matmul(out_ap, w_hi, v_lo, start=False, stop=False)
            return nc.tensor.matmul(out_ap, w_lo, v_hi, start=False, stop=stop)

        block = ctx.enter_context(nc.Block())

        @block.sync
        def _(sp):
            def load_expert(n):
                landed = expert_landed[n]
                gate, up, down = ((sw_gate, sw_up, sw_down) if n == 0
                                  else (we_gate[n - 1], we_up[n - 1], we_down[n - 1]))
                s = n % STAGE
                if n >= STAGE:
                    sp.wait_ge(expert_lo, n - STAGE + 1)
                sp.dma_start(raw_gu[:, s, 0, :], gate).then_inc(landed, 16)
                sp.dma_start(raw_gu[:, s, 1, :], up).then_inc(landed, 16)
                if n == 0:
                    sp.wait_ge(stage_cleared, 1)
                whole = FD // P * P
                sp.dma_start(raw_down[:, s, 0:FD // P, :],
                             down[0:whole, :].rearrange("(j p) e -> p j e", p=P)).then_inc(landed, 16)
                sp.dma_start(raw_down[0:FD - whole, s, FD // P, :], down[whole:FD, :]).then_inc(landed, 16)

            x_tok = x[0].rearrange("(i p) e -> p i e", p=P)
            sp.dma_start(x_res[:, 0:TILES, :], x_tok[:, 0:TILES, :]).then_inc(x_in_landed[0], 16)
            for i, w in enumerate((Wq, Wk, Wv)):
                sp.dma_start(raw_qkv[:, i, :], w).then_inc(attn_w_landed, 16)
            load_expert(0)
            for c in range(1, CHUNKS):
                sp.dma_start(x_res[:, c * TILES:(c + 1) * TILES, :],
                             x_tok[:, c * TILES:(c + 1) * TILES, :]).then_inc(x_in_landed[c], 16)
            for n in range(1, NX):
                load_expert(n)
            out_tok = out[0].rearrange("(i p) e -> p i e", p=P)
            with sp.Fori(0, CHUNKS) as c:
                sp.wait_ge(x_out_made, c + 1)
                sp.dma_start(out_tok[:, tiles(c), :], x_out[:]).then_inc(out_stored, 16)
            sp.wait_ge(out_stored, 16 * CHUNKS)

        @block.gpsimd
        def _(pool):
            nc.gpsimd.memset(ident[:], 0.0)
            nc.gpsimd.memset(head_of[:], 1.0)
            nc.gpsimd.memset(head_rows[:], 1.0)
            nc.gpsimd.memset(pick_expert_f, 0.0).then_inc(pool_const, 1)
            pool.wait_ge(pool_const, 1)
            nc.gpsimd.affine_select(out=ident[:], in_=ident[:], compare_op=ALU.not_equal, fill=1.0,
                                    base=0, pattern=[[-1, P]], channel_multiplier=1)
            nc.gpsimd.affine_select(out=head_of[:], in_=head_of[:], compare_op=ALU.is_ge, fill=0.0,
                                    base=0, pattern=[[-D, HEADS]], channel_multiplier=1)
            nc.gpsimd.affine_select(out=head_rows[:], in_=head_rows[:], compare_op=ALU.is_ge, fill=0.0,
                                    base=0, pattern=[[1, P]], channel_multiplier=-D)
            nc.gpsimd.affine_select(out=pick_expert_f, in_=pick_expert_f, compare_op=ALU.not_equal,
                                    fill=1.0, base=0, pattern=[[-1, NE], [0, P]],
                                    channel_multiplier=1).then_inc(pool_const, 1)
            pool.wait_ge(pool_const, 2)
            nc.gpsimd.affine_select(out=head_of[:], in_=head_of[:], compare_op=ALU.is_ge, fill=0.0,
                                    base=D - 1, pattern=[[D, HEADS]], channel_multiplier=-1)
            nc.gpsimd.affine_select(out=head_rows[:], in_=head_rows[:], compare_op=ALU.is_ge, fill=0.0,
                                    base=D - 1, pattern=[[-1, P]], channel_multiplier=D)
            nc.gpsimd.affine_select(out=pick_expert_f, in_=pick_expert_f, compare_op=ALU.not_equal,
                                    fill=1.0, base=-LO, pattern=[[-1, NE], [0, P]],
                                    channel_multiplier=1).then_inc(consts_made, 1)
            nc.gpsimd.memset(raw_down[:], 0.0).then_inc(stage_cleared, 1)
            nc.gpsimd.memset(cw_rows[:].bitcast(F32), 0.0).then_inc(cw_cleared, 1)
            for e in range(NE):
                last = nc.gpsimd.memset(order[:, :, e:e + 1], float(NE - e))
            last.then_inc(picks_made, 1)

            def attention(s, c):
                if 5 <= s < 5 + D:
                    v = s - 5
                    pool.wait_ge(scanned, D * c + v + 1)
                    pool.nop(nofuse=True)
                    nc.gpsimd.tensor_copy(carry[:, v:v + 1], state[:, v % 2, CHUNK - 1:CHUNK]).then_inc(carried, 1)
                    pool.wait_ge(qs_hi_made, D * c + v + 1)
                    nc.gpsimd.tensor_tensor(qs_lo[:, v % 2, :], qs[:, v % 2, :], qs_hi[:, v % 2, :].bitcast(F32),
                                            ALU.subtract).then_inc(qs_lo_made, 1)

            def split_low(n, c):
                pool.wait_ge(h_hi_made, STEPS * c + n + 1)
                nc.gpsimd.tensor_tensor(h_lo[:, n % 3, :], h[:, n % 2, :], h_hi[:, n % 3, :].bitcast(F32),
                                        ALU.subtract).then_inc(h_lo_made, 1)

            def expert_low(n):
                pool.wait_ge(expert_hi, n + 1)
                s = n % STAGE
                nc.gpsimd.tensor_tensor(gu_lo[:, n], raw_gu[:, s], gu_hi[:, n].bitcast(F32), ALU.subtract)
                nc.gpsimd.tensor_tensor(down_lo[:, n], raw_down[:, s], down_hi[:, n].bitcast(F32),
                                        ALU.subtract).then_inc(expert_lo, 1)

            for s in range(STEPS):
                attention(s, 0)
                if s % 2 == 0 and s // 2 < NX:
                    expert_low(s // 2)
            def both(c):
                for n in range(STEPS):
                    if n >= 1:
                        split_low(n - 1, c)
                    attention(n, c + 1)
                split_low(STEPS - 1, c)

            both(0)
            with pool.Fori(1, CHUNKS - 1) as c:
                both(c)
            for n in range(STEPS):
                split_low(n, CHUNKS - 1)

        @block.scalar
        def _(act):
            act.dma_start(raw_fg1[:, 0, :], Wf1).then_inc(small_w_landed, 16)
            act.dma_start(raw_fg1[:, 1, :], Wg1).then_inc(small_w_landed, 16)
            act.dma_start(raw_fg2[:, 0, :], Wf2).then_inc(small_w_landed, 16)
            act.dma_start(raw_fg2[:, 1, :], Wg2).then_inc(small_w_landed, 16)
            act.dma_start(raw_route[:], gate_w).then_inc(small_w_landed, 16)
            act.dma_start(norm_w[:], norm_weight.rearrange("(p a) -> p a", a=1)).then_inc(small_w_landed, 16)
            act.dma_start(w_out[:], Wo).then_inc(small_w_landed, 16)

            def copy(dst, src):
                return nc.scalar.activation(dst, src, ACT.Copy)

            def attention(s, c):
                if s == 1:
                    act.wait_ge(xn_turned, c + 1)
                    atleast(act, v_spread, D * c)
                    copy(xn_hi[:], a_ps[:]).then_inc(xn_hi_made, 1)
                if s == 2:
                    act.wait_ge(qk_projected, c + 1)
                    atleast(act, qs_made, D * c)
                    nc.scalar.activation(q[:], a_ps[:], ACT.Silu)
                    nc.scalar.activation(k[:], o_ps[:], ACT.Silu).then_inc(qk_made, 1)
                if s == 3:
                    act.wait_ge(fg_projected, c + 1)
                    atleast(act, og_made, c)
                    nc.scalar.activation(f[:], a_ps[:], ACT.Sigmoid)
                    nc.scalar.activation(g[:], o_ps[:], ACT.Sigmoid).then_inc(fg_made, 1)
                if 5 <= s < 5 + D:
                    v = s - 5
                    act.wait_ge(qs_made, D * c + v + 1)
                    atleast(act, qs_summed, D * c + v - 1)
                    copy(qs_hi[:, v % 2, :], qs[:, v % 2, :]).then_inc(qs_hi_made, 1)
                if s == 14:
                    act.wait_ge(og_made, c + 1)
                    atleast(act, sq_summed, c)
                    nc.scalar.activation(turns[:], og[:], ACT.Square).then_inc(sq_made, 1)
                if s == 15:
                    act.wait_ge(rs_turned, c + 1)
                    atleast(act, rs_spread, c)
                    copy(rs_rows[:], a_ps[0:HEADS, :]).then_inc(rs_copied, 1)
                if s == 21:
                    act.wait_ge(x2_turned, c + 1)
                    atleast(act, down_done, STEPS * (c - 1))
                    half = ff_cols(c)
                    copy(turns[:], a_ps[:])
                    copy(ff[:, half], a_ps[:])
                    copy(ff_hi[:, half], a_ps[:]).then_inc(x2_copied, 1)
                if s == 23:
                    act.wait_ge(z_made, c + 1)
                    nc.scalar.activation(ez[:], z[:], ACT.Exp).then_inc(exp_made, 1)
                if s == 25:
                    act.wait_ge(cw_turned, c + 1)
                    if isinstance(c, int):
                        act.wait_ge(cw_cleared, 1)
                    copy(cw_rows[0:NE, ff_cols(c)], a_ps[0:NE, :]).then_inc(cw_hi_made, 1)

            def high(n, c):
                act.wait_ge(h_made, STEPS * c + n + 1)
                atleast(act, down_done, STEPS * c + max(n - 2, 0))
                copy(h_hi[:, n % 3, :], h[:, n % 2, :]).then_inc(h_hi_made, 1)

            def feed_forward(n, c):
                act.wait_ge(gate_done, STEPS * c + n + 1)
                atleast(act, h_made, STEPS * c + max(n - 1, 0))
                r = ROWS[n % NJ][1]
                nc.scalar.activation(sg[0:r, n % 2, :], gate_ps[n % 2][0:r, :], ACT.Silu).then_inc(silu_done, 1)
                if n >= 1:
                    high(n - 1, c)
                e, j = divmod(n, NJ)
                if j == 1 and e < NE:
                    act.wait_ge(xs_made, NE * c + e + 1)
                    atleast(act, up_done, STEPS * c + max(NJ * (e - 1) + NJ, 0) if e >= 2 else STEPS * c)
                    copy(xs_hi[:, e % 2, :], xs[:, e % 2, :]).then_inc(xs_hi_made, 1)

            def feed_forward_end(c):
                high(STEPS - 1, c)
                act.wait_ge(down_done, STEPS * (c + 1))
                atleast(act, y_turned, c)
                copy(y_t[:], y_ps[:]).then_inc(y_copied, 1)

            def expert_high(n):
                act.wait_ge(expert_landed[n], 64)
                if n == 0:
                    act.wait_ge(stage_cleared, 1)
                s = n % STAGE
                copy(gu_hi[:, n], raw_gu[:, s])
                copy(down_hi[:, n], raw_down[:, s]).then_inc(expert_hi, 1)

            for s in range(STEPS):
                attention(s, 0)
                if s % 2 == 0 and s // 2 < NX:
                    expert_high(s // 2)
            def both(c):
                for n in range(STEPS):
                    feed_forward(n, c)
                    attention(n, c + 1)
                feed_forward_end(c)

            both(0)
            with act.Fori(1, CHUNKS - 1) as c:
                both(c)
            for n in range(STEPS):
                feed_forward(n, CHUNKS - 1)
            feed_forward_end(CHUNKS - 1)

        @block.vector
        def _(dve):
            Y_LINKS = 3 + 2 + 3 * NEWTON_STEPS
            per_chunk = {y_chain: Y_LINKS}
            done = {}

            def link(chain, c, ins):
                done[chain] = done.get(chain, 0) + 1
                ins.then_inc(chain, 1)
                dve.wait_ge(chain, c * per_chunk.get(chain, 0) + done[chain])

            def finish(chain):
                per_chunk[chain] = done.pop(chain)

            def rsqrt(chain, c, n):
                v, y, t, mh = var_eps[:, 0:n], rs[:, 0:n], newton[:, 0:n], minus_half[:, 0:n]
                nc.vector.tensor_scalar(mh, v, -0.5, None, ALU.mult)
                link(chain, c, nc.vector.tensor_scalar(t.bitcast(I32), v.bitcast(I32), 1, None,
                                                       ALU.logical_shift_right))
                link(chain, c, nc.vector.tensor_scalar(y.bitcast(I32), t.bitcast(I32), -1.0, float(RSQRT_MAGIC),
                                                       ALU.mult, ALU.add))
                for step in range(NEWTON_STEPS):
                    link(chain, c, nc.vector.tensor_tensor(t, y, y, ALU.mult))
                    link(chain, c, nc.vector.tensor_tensor(t, t, mh, ALU.mult))
                    last = nc.vector.scalar_tensor_tensor(y, t, 1.5, y, ALU.add, ALU.mult)
                    if step < NEWTON_STEPS - 1:
                        link(chain, c, last)
                return last

            def tile_stats(chain, c, src, st, mom, read=None):
                for i in range(TILES):
                    last = nc.vector.bn_stats(st[:, i, :], src(i))
                link(chain, c, last)
                dve.nop(nofuse=True)
                for i in range(TILES):
                    last = nc.vector.bn_aggr(mom[:, i, :], st[:, i, :])
                link(chain, c, last)
                link(chain, c, nc.vector.tensor_scalar(var_eps[:, 0:TILES], mom[:, :, 1], EPS, None, ALU.add))

            def normalise(dst, src, mom):
                for i in range(TILES):
                    last = nc.vector.tensor_scalar(dst[:, i, :], src(i), mom[:, i, 0:1], rs[:, i:i + 1],
                                                   ALU.subtract, ALU.mult)
                return last

            def spread(ap):
                return ap.unsqueeze(2).to_broadcast([P, TILES, NE])

            def attention(s, c):
                def lk(ins):
                    link(attn_chain, c, ins)

                if s == 0:
                    if isinstance(c, int):
                        dve.wait_ge(x_in_landed[c], 16)
                    tile_stats(attn_chain, c, lambda i: tile_of(x_res, c, i), stats, moments)
                    lk(rsqrt(attn_chain, c, TILES))
                    atleast(dve, xn_turned, c)
                    normalise(xn, lambda i: tile_of(x_res, c, i), moments).then_inc(xn_made, 1)
                if s == 1:
                    dve.wait_ge(xn_hi_made, c + 1)
                    nc.vector.tensor_tensor(xn_lo[:], a_ps[:], xn_hi[:].bitcast(F32),
                                            ALU.subtract).then_inc(xn_lo_made, 1)
                if 4 <= s < 4 + D:
                    v = s - 4
                    if v == 0:
                        dve.wait_ge(qk_made, c + 1)
                        dve.wait_ge(fg_made, c + 1)
                    dve.wait_ge(v_spread, D * c + v + 1)
                    nc.vector.tensor_tensor(a_ps[:], a_ps[:], k[:], ALU.mult).then_inc(kv_made, 1)
                    dve.wait_ge(kv_made, D * c + v + 1)
                    atleast(dve, carried, D * c + v - 1)
                    first_state = 0.0 if isinstance(c, int) and c == 0 else carry[:, v:v + 1]
                    nc.vector.tensor_tensor_scan(state[:, v % 2, :], f[:], a_ps[:], first_state,
                                                 ALU.mult, ALU.add).then_inc(scanned, 1)
                    dve.wait_ge(scanned, D * c + v + 1)
                    atleast(dve, qs_lo_made, D * c + v - 1)
                    nc.vector.tensor_tensor(qs[:, v % 2, :], state[:, v % 2, :], q[:], ALU.mult).then_inc(qs_made, 1)
                if s == 13:
                    dve.wait_ge(qs_summed, D * c + D)
                    nc.vector.scalar_tensor_tensor(og[:], o_ps[:], SCALE, g[:], ALU.mult,
                                                   ALU.mult).then_inc(og_made, 1)
                if s == 14:
                    dve.wait_ge(sq_summed, c + 1)
                    lk(nc.vector.tensor_scalar(var_eps[:], a_ps[:, 0:TILES * HEADS], 1.0 / D, EPS,
                                               ALU.mult, ALU.add))
                    rsqrt(attn_chain, c, TILES * HEADS).then_inc(rs_made, 1)
                if s == 16:
                    dve.wait_ge(rs_spread, c + 1)
                    nc.vector.scalar_tensor_tensor(turns[:], og[:], norm_w[:], o_ps[:], ALU.mult,
                                                   ALU.mult).then_inc(on_made, 1)
                if s == 17:
                    dve.wait_ge(attn_projected, c + 1)
                    tile_stats(attn_chain, c, lambda i: a_tok[:, i, :], stats, moments)
                if s == 18:
                    lk(rsqrt(attn_chain, c, TILES))
                    lk(normalise(xn, lambda i: a_tok[:, i, :], moments))
                    lk(nc.vector.tensor_tensor(x_res[:, tiles(c), :], xn[:], x_res[:, tiles(c), :],
                                               ALU.add))
                if s == 19:
                    tile_stats(attn_chain, c, lambda i: tile_of(x_res, c, i), stats, moments)
                if s == 20:
                    lk(rsqrt(attn_chain, c, TILES))
                    normalise(xn, lambda i: tile_of(x_res, c, i), moments).then_inc(x2n_made, 1)
                if s == 21:
                    dve.wait_ge(x2_copied, c + 1)
                    half = ff_cols(c)
                    nc.vector.tensor_tensor(ff_lo[:, half], a_ps[:],
                                            ff_hi[:, half].bitcast(F32), ALU.subtract).then_inc(x2_lo_made, 1)
                if s == 22:
                    dve.wait_ge(logits_made, c + 1)
                    logits = o_ps[:, 0:TILES * NE].rearrange("p (i e) -> p i e", e=NE)
                    lk(nc.vector.tensor_reduce(top[:, 0, :], logits, AX_X, ALU.max))
                    nc.vector.tensor_tensor(z[:], logits, spread(top[:, 0, :]), ALU.subtract).then_inc(z_made, 1)
                if s == 23:
                    dve.wait_ge(exp_made, c + 1)
                    lk(nc.vector.tensor_reduce(top[:, 1, :], ez[:], AX_X, ALU.add))
                    lk(nc.vector.reciprocal(top[:, 2, :], top[:, 1, :]))
                    lk(nc.vector.tensor_tensor(prob[:], ez[:], spread(top[:, 2, :]), ALU.mult))
                    place(lk, prob, top[:, 3, :], top[:, 4, :], first)
                    lk(nc.vector.scalar_tensor_tensor(rest[:], first[:], -2.0, prob[:], ALU.mult, ALU.add))
                if s == 24:
                    place(lk, rest, top[:, 5, :], top[:, 6, :], second)
                    lk(nc.vector.tensor_tensor(cand[:], first[:], second[:], ALU.add))
                    lk(nc.vector.tensor_tensor(cand[:], cand[:], prob[:], ALU.mult))
                    lk(nc.vector.tensor_reduce(top[:, 7, :], cand[:], AX_X, ALU.add))
                    lk(nc.vector.tensor_scalar(top[:, 0, :], top[:, 7, :], 1e-20, None, ALU.add))
                    lk(nc.vector.reciprocal(top[:, 1, :], top[:, 0, :]))
                    nc.vector.tensor_tensor(cw[:], cand[:], spread(top[:, 1, :]), ALU.mult).then_inc(cw_made, 1)
                if s == 25:
                    dve.wait_ge(cw_hi_made, c + 1)
                    nc.vector.tensor_tensor(cw_rows[LO:LO + NE, ff_cols(c)], a_ps[0:NE, :],
                                            cw_rows[0:NE, ff_cols(c)].bitcast(F32),
                                            ALU.subtract).then_inc(cw_lo_made, 1)

            def place(lk, values, largest, rank, mask):
                lk(nc.vector.tensor_reduce(largest, values[:], AX_X, ALU.max))
                lk(nc.vector.tensor_tensor(cand[:], values[:], spread(largest), ALU.is_equal))
                lk(nc.vector.tensor_tensor(cand[:], cand[:], order[:], ALU.mult))
                lk(nc.vector.tensor_reduce(rank, cand[:], AX_X, ALU.max))
                lk(nc.vector.tensor_tensor(mask[:], cand[:], spread(rank), ALU.is_equal))

            def feed_forward(n, c):
                r = ROWS[n % NJ][1]
                dve.wait_ge(silu_done, STEPS * c + n + 1)
                dve.wait_ge(up_done, STEPS * c + n + 1)
                atleast(dve, h_lo_made, STEPS * c + max(n - 1, 0))
                nc.vector.tensor_tensor(h[0:r, n % 2, :], sg[0:r, n % 2, :], up_ps[n % 2][0:r, :],
                                        ALU.mult).then_inc(h_made, 1)
                e, j = divmod(n, NJ)
                if j == 0 and e < NE:
                    dve.wait_ge(cw_spread, NE * c + e + 1)
                    nc.vector.tensor_tensor(xs[:, e % 2, :], ff[:, ff_cols(c)], w_ps[:],
                                            ALU.mult).then_inc(xs_made, 1)
                if j == 1 and e < NE:
                    dve.wait_ge(xs_hi_made, NE * c + e + 1)
                    nc.vector.tensor_tensor(xs_lo[:, e % 2, :], xs[:, e % 2, :], xs_hi[:, e % 2, :].bitcast(F32),
                                            ALU.subtract).then_inc(xs_lo_made, 1)

            def feed_forward_end(c):
                dve.wait_ge(y_turned, c + 1)
                tile_stats(y_chain, c, lambda i: w_tok[:, i, :], y_stats, y_mom)
                link(y_chain, c, rsqrt(y_chain, c, TILES))
                atleast(dve, out_stored, 16 * c)
                normalise(x_out, lambda i: w_tok[:, i, :], y_mom).then_inc(y_read, 1)
                dve.wait_ge(y_read, c + 1)
                nc.vector.tensor_tensor(x_out[:], x_out[:], x_res[:, tiles(c), :], ALU.add).then_inc(x_out_made, 1)

            dve.wait_ge(attn_w_landed, 48)
            v_cols = raw_qkv[:, 2, :].rearrange("p (h v) -> p v h", v=D).unsqueeze(3).to_broadcast([P, D, HEADS, D])
            vh = vrep_hi[:].rearrange("p v (h k) -> p v h k", k=D)
            vl = vrep_lo[:].rearrange("p v (h k) -> p v h k", k=D)
            nc.vector.tensor_copy(proj_hi[:, 0:2, :], raw_qkv[:, 0:2, :])
            nc.vector.tensor_copy(vh, v_cols).then_inc(attn_w_hi, 1)
            dve.wait_ge(attn_w_hi, 1)
            nc.vector.tensor_tensor(proj_lo[:, 0:2, :], raw_qkv[:, 0:2, :], proj_hi[:, 0:2, :].bitcast(F32),
                                    ALU.subtract)
            nc.vector.tensor_tensor(vl, v_cols, vh.bitcast(F32), ALU.subtract).then_inc(attn_w_ready, 1)
            dve.wait_ge(small_turned, 1)
            nc.vector.tensor_copy(fg1_t[:], a_ps[0:D, 0:2 * E].rearrange("d (g e) -> d g e", g=2))
            nc.vector.tensor_copy(route_t[:], a_ps[:, 2 * E:2 * E + NE]).then_inc(small_copied, 1)
            dve.wait_ge(fg_composed, 1)
            fg = o_ps[:, 0:2 * E].rearrange("p (g e) -> p g e", g=2)
            nc.vector.tensor_copy(proj_hi[:, 2:4, :], fg).then_inc(attn_w_hi, 1)
            dve.wait_ge(attn_w_hi, 2)
            nc.vector.tensor_tensor(proj_lo[:, 2:4, :], fg, proj_hi[:, 2:4, :].bitcast(F32),
                                    ALU.subtract).then_inc(attn_w_ready, 1)
            nc.vector.memset(pick_v[:].bitcast(F32), 0.0).then_inc(pick_copied, 1)
            dve.wait_ge(pick_copied, 1)
            dve.wait_ge(consts_made, 1)
            for v in range(D):
                nc.vector.tensor_copy(pick_v[:, v, :].rearrange("p (h w) -> p h w", w=D)[:, :, v], head_of[:])
            nc.vector.tensor_copy(pick_expert[:], pick_expert_f).then_inc(pick_copied, 1)
            dve.wait_ge(picks_made, 1)

            for s in range(STEPS):
                attention(s, 0)
            finish(attn_chain)
            for c in range(1, CHUNKS):
                dve.wait_ge(x_in_landed[c], 16)
            def both(c):
                for n in range(STEPS):
                    feed_forward(n, c)
                    attention(n, c + 1)
                feed_forward_end(c)
                done.clear()

            both(0)
            with dve.Fori(1, CHUNKS - 1) as c:
                both(c)
            for n in range(STEPS):
                feed_forward(n, CHUNKS - 1)
            feed_forward_end(CHUNKS - 1)
            assert done[y_chain] == Y_LINKS

        @block.tensor
        def _(pe):
            def turn(dst, src, rows=P):
                return nc.tensor.transpose(dst, src, ident[0:rows, 0:rows])

            def attention(s, c):
                if s == 1:
                    pe.wait_ge(xn_made, c + 1)
                    atleast(pe, cw_lo_made, c)
                    for i in range(TILES):
                        last = turn(a_tok[:, i, :], xn[:, i, :])
                    last.then_inc(xn_turned, 1)
                if s == 2:
                    pe.wait_ge(xn_lo_made, c + 1)
                    if isinstance(c, int):
                        pe.wait_ge(attn_w_ready, 1)
                    three(a_ps[:], proj_hi[:, 0, :], proj_lo[:, 0, :], xn_hi[:], xn_lo[:])
                    atleast(pe, z_made, c)
                    three(o_ps[:], proj_hi[:, 1, :], proj_lo[:, 1, :], xn_hi[:], xn_lo[:]).then_inc(qk_projected, 1)
                if s == 3:
                    if isinstance(c, int):
                        pe.wait_ge(attn_w_ready, 2)
                    pe.wait_ge(qk_made, c + 1)
                    three(a_ps[:], proj_hi[:, 2, :], proj_lo[:, 2, :], xn_hi[:], xn_lo[:])
                    three(o_ps[:], proj_hi[:, 3, :], proj_lo[:, 3, :], xn_hi[:], xn_lo[:]).then_inc(fg_projected, 1)
                if 4 <= s < 4 + D:
                    v = s - 4
                    if v == 0:
                        pe.wait_ge(fg_made, c + 1)
                    atleast(pe, scanned, D * c + v)
                    three(a_ps[:], vrep_hi[:, v, :], vrep_lo[:, v, :], xn_hi[:], xn_lo[:]).then_inc(v_spread, 1)
                if 6 <= s < 6 + D:
                    v = s - 6
                    if v == 0 and isinstance(c, int):
                        pe.wait_ge(pick_copied, 2)
                    pe.wait_ge(qs_lo_made, D * c + v + 1)
                    nc.tensor.matmul(o_ps[:], pick_v[:, v, :], qs_hi[:, v % 2, :], start=(v == 0), stop=False)
                    last = nc.tensor.matmul(o_ps[:], pick_v[:, v, :], qs_lo[:, v % 2, :], start=False,
                                            stop=(v == D - 1))
                    last.then_inc(qs_summed, 1)
                if s == 14:
                    pe.wait_ge(sq_made, c + 1)
                    pe.wait_ge(scanned, D * c + D)
                    for i in range(TILES):
                        last = nc.tensor.matmul(a_ps[:, i * HEADS:(i + 1) * HEADS], turns[:, i * P:(i + 1) * P],
                                                head_of[:], start=True, stop=True)
                    last.then_inc(sq_summed, 1)
                if s == 15:
                    pe.wait_ge(rs_made, c + 1)
                    for i in range(TILES):
                        last = turn(a_ps[0:HEADS, i * P:(i + 1) * P], rs[:, i * HEADS:(i + 1) * HEADS])
                    last.then_inc(rs_turned, 1)
                if s == 16:
                    pe.wait_ge(rs_copied, c + 1)
                    pe.wait_ge(og_made, c + 1)
                    nc.tensor.matmul(o_ps[:], head_rows[:], rs_rows[:], start=True, stop=True).then_inc(rs_spread, 1)
                if s == 17:
                    pe.wait_ge(on_made, c + 1)
                    for i in range(TILES):
                        last = nc.tensor.matmul(a_tok[:, i, :], turns[:, i * P:(i + 1) * P], w_out[:],
                                                start=True, stop=True)
                    last.then_inc(attn_projected, 1)
                if s == 21:
                    pe.wait_ge(x2n_made, c + 1)
                    for i in range(TILES):
                        last = turn(a_tok[:, i, :], xn[:, i, :])
                    last.then_inc(x2_turned, 1)
                if s == 22:
                    pe.wait_ge(x2_copied, c + 1)
                    for i in range(TILES):
                        last = nc.tensor.matmul(o_ps[:, i * NE:(i + 1) * NE], turns[:, i * P:(i + 1) * P],
                                                route_t[:], start=True, stop=True)
                    last.then_inc(logits_made, 1)
                if s == 25:
                    pe.wait_ge(cw_made, c + 1)
                    pe.wait_ge(x2_lo_made, c + 1)
                    for i in range(TILES):
                        last = turn(a_ps[0:NE, i * P:(i + 1) * P], cw[:, i, :])
                    last.then_inc(cw_turned, 1)

            def down(n, c):
                r = ROWS[n % NJ][1]
                e, j = divmod(n, NJ)
                pe.wait_ge(h_lo_made, STEPS * c + n + 1)
                if n == 0:
                    atleast(pe, y_copied, c)
                three(y_ps[:], down_hi[0:r, e, j, :], down_lo[0:r, e, j, :], h_hi[0:r, n % 3, :],
                      h_lo[0:r, n % 3, :], start=(n == 0), stop=(n == STEPS - 1)).then_inc(down_done, 1)

            def feed_forward(n, c):
                e, j = divmod(n, NJ)
                row, r = ROWS[j]
                half = ff_cols(c)
                x_hi, x_lo = ff_hi[:, half], ff_lo[:, half]
                if n == 0:
                    pe.wait_ge(x2_lo_made, c + 1)
                    pe.wait_ge(cw_lo_made, c + 1)
                    atleast(pe, y_read, c)
                if j == 0:
                    pe.wait_ge(expert_lo, e + 1)
                if j == 0 and e < NE:
                    if e >= 1:
                        pe.wait_ge(xs_made, NE * c + e)
                    pe.nop(nofuse=True)
                    nc.tensor.matmul(w_ps[:], pick_expert[:, e, :], cw_rows[:, ff_cols(c)],
                                     start=True, stop=True).then_inc(cw_spread, 1)
                atleast(pe, silu_done, STEPS * c + max(n - 1, 0))
                three(gate_ps[n % 2][0:r, :], gu_hi[:, e, 0, row:row + r], gu_lo[:, e, 0, row:row + r],
                      x_hi, x_lo).then_inc(gate_done, 1)
                if e >= 1:
                    pe.wait_ge(xs_lo_made, NE * c + e)
                    u_hi, u_lo = xs_hi[:, (e - 1) % 2, :], xs_lo[:, (e - 1) % 2, :]
                else:
                    u_hi, u_lo = x_hi, x_lo
                atleast(pe, h_made, STEPS * c + max(n - 1, 0))
                three(up_ps[n % 2][0:r, :], gu_hi[:, e, 1, row:row + r], gu_lo[:, e, 1, row:row + r],
                      u_hi, u_lo).then_inc(up_done, 1)
                if n >= 2:
                    down(n - 2, c)

            def feed_forward_end(c):
                down(STEPS - 2, c)
                down(STEPS - 1, c)
                pe.wait_ge(y_copied, c + 1)
                pe.wait_ge(xs_made, NE * (c + 1))
                for i in range(TILES):
                    last = turn(w_tok[:, i, :], y_t[:, i * P:(i + 1) * P])
                last.then_inc(y_turned, 1)

            pe.wait_ge(small_w_landed, 16 * 7)
            pe.wait_ge(consts_made, 1)
            for i in range(2):
                turn(a_ps[0:D, i * E:(i + 1) * E], raw_fg1[:, i, :])
            turn(a_ps[:, 2 * E:2 * E + NE], raw_route[:], NE).then_inc(small_turned, 1)
            pe.wait_ge(small_copied, 1)
            for i in range(2):
                last = nc.tensor.matmul(o_ps[:, i * E:(i + 1) * E], fg1_t[:, i, :], raw_fg2[:, i, :],
                                        start=True, stop=True)
            last.then_inc(fg_composed, 1)

            for s in range(STEPS):
                attention(s, 0)
            def both(c):
                for n in range(STEPS):
                    feed_forward(n, c)
                    attention(n, c + 1)
                feed_forward_end(c)

            both(0)
            with pe.Fori(1, CHUNKS - 1) as c:
                both(c)
            for n in range(STEPS):
                feed_forward(n, CHUNKS - 1)
            feed_forward_end(CHUNKS - 1)


_INS = ["x", "Wq", "Wk", "Wv", "Wo", "Wf1", "Wf2", "Wg1", "Wg2", "norm_weight"]
_FFN = ["gate_w", "we_gate", "we_up", "we_down", "sw_gate", "sw_up", "sw_down"]


def kernel(**inputs):
    import numpy as np
    import concourse.bacc as bacc
    from concourse.bass_utils import run_bass_kernel_spmd

    nc = bacc.Bacc("TRN2", target_bir_lowering=False, num_devices=1)
    arrays, args = {}, []
    for name in ["L0_attn_" + n for n in _INS] + ["L0_ffn_" + n for n in _FFN]:
        a = np.ascontiguousarray(inputs[name])
        arrays[f"in_{name}"] = a
        args.append(nc.dram_tensor(f"in_{name}", a.shape, mybir.dt.from_np(a.dtype), kind="ExternalInput").ap())
    shape = inputs["L0_attn_x"].shape
    out = nc.dram_tensor("out_0", shape, F32, kind="ExternalOutput").ap()
    build(nc, *args, out)
    r = run_bass_kernel_spmd(nc, [arrays], core_ids=[0])
    return r.results[0]["out_0"]
```

```python
from contextlib import ExitStack

import concourse.bass as bass
from concourse import mybir

P = 128
F32 = mybir.dt.float32
F32R = mybir.dt.float32r
I32 = mybir.dt.int32
ALU = mybir.AluOpType
ACT = mybir.ActivationFunctionType
AX_X = mybir.AxisListType.X

CHUNK = 512
TILES = CHUNK // P
EPS = 1e-5
RSQRT_MAGIC = 0x5F3759DF
NEWTON_STEPS = 3


def build(nc, x, Wq, Wk, Wv, Wo, Wf1, Wf2, Wg1, Wg2, norm_weight, gate_w,
          we_gate, we_up, we_down, sw_gate, sw_up, sw_down, out):
    _, TOKENS, E = x.shape
    D = Wf1.shape[1]
    HEADS = E // D
    NE, _, FD = we_gate.shape
    NX = NE + 1
    CHUNKS = TOKENS // CHUNK
    SCALE = float(D) ** -0.5
    ROWS = [(j, min(P, FD - j)) for j in range(0, FD, P)]
    NJ = len(ROWS)
    STEPS = NX * NJ
    LO = 32
    STAGE = 2
    HEAD = 5
    EARLY_AT = {0: [0, 1], 1: [2], 2: [3], 4: [4], 7: [5], 8: [6], 10: [7], 12: [8], 13: [9], 16: [10],
                18: [11], 19: [12], 20: [13]}
    LATE_AT = {1: [14], 2: [15], 3: [16], 5: [17], 6: [18], 8: [19], 9: [20], 11: [21], 12: [22], 15: [23],
               17: [24], 19: [25]}
    END_AT = {STEPS - HEAD + 1: [0], STEPS - HEAD + 2: [1], STEPS - HEAD + 3: [2], STEPS - HEAD + 4: [3]}
    EARLY, LATE = range(0, 14), range(14, 26)
    LATE_STEP = {stage: slot + HEAD for slot, stages in LATE_AT.items() for stage in stages}
    assert E == P and TOKENS % CHUNK == 0 and STEPS % 3 == 0 and NE % 2 == 0

    with ExitStack() as ctx:
        def sb(name, shape, dt=F32):
            return ctx.enter_context(nc.sbuf_tensor(name, shape, dt))

        def bank(name):
            return ctx.enter_context(nc.psum_tensor(name, [P, CHUNK], F32))

        def sem(name):
            return ctx.enter_context(nc.semaphore(name))

        w_out = sb("w_out", [P, E])
        raw_fg1 = sb("raw_fg1", [P, 2, D])
        raw_fg2 = sb("raw_fg2", [D, 2, E])
        raw_route = sb("raw_route", [NE, E])
        norm_w = sb("norm_w", [P, 1])
        raw_gu = sb("raw_gu", [P, STAGE, 2, FD])
        raw_down = sb("raw_down", [P, STAGE, NJ, E])
        proj_hi = sb("proj_hi", [P, 4, E], F32R)
        proj_lo = sb("proj_lo", [P, 4, E], F32R)
        vrep_hi = sb("vrep_hi", [P, D, E], F32R)
        vrep_lo = sb("vrep_lo", [P, D, E], F32R)
        fg1_t = sb("fg1_t", [D, 2, E])
        route_t = sb("route_t", [P, NE])
        gu_hi = sb("gu_hi", [P, NX, 2, FD], F32R)
        gu_lo = sb("gu_lo", [P, NX, 2, FD], F32R)
        down_hi = sb("down_hi", [P, NX, NJ, E], F32R)
        down_lo = sb("down_lo", [P, NX, NJ, E], F32R)
        ident = sb("ident", [P, P])
        head_of = sb("head_of", [P, HEADS])
        head_rows = sb("head_rows", [HEADS, P])
        pick_v = sb("pick_v", [P, D, E], F32R)
        pick_expert = sb("pick_expert", [LO + NE, NE, P], F32R)
        x_res = sb("x_res", [P, TOKENS // P, E])
        stats = sb("stats", [P, TOKENS // P, 6])
        x_mom = sb("x_mom", [P, TOKENS // P, 2])
        x_rs = sb("x_rs", [P, TOKENS // P])
        moments = sb("moments", [P, TILES, 2])
        var_eps = sb("var_eps", [P, TILES * HEADS])
        minus_half = sb("minus_half", [P, TILES * HEADS])
        rs = sb("rs", [P, TILES * HEADS])
        newton = sb("newton", [P, TILES * HEADS])
        xn = sb("xn", [P, TILES, E])
        an = sb("an", [P, TILES, E])
        xn_hi = sb("xn_hi", [P, CHUNK], F32R)
        xn_lo = sb("xn_lo", [P, CHUNK], F32R)
        q = sb("q", [P, CHUNK])
        k = sb("k", [P, CHUNK])
        f = sb("f", [P, CHUNK])
        g = sb("g", [P, CHUNK])
        state = sb("state", [P, 2, CHUNK])
        carry = sb("carry", [P, D])
        qs = sb("qs", [P, 2, CHUNK])
        qs_hi = sb("qs_hi", [P, 2, CHUNK], F32R)
        qs_lo = sb("qs_lo", [P, 2, CHUNK], F32R)
        og = sb("og", [P, CHUNK])
        rs_rows = sb("rs_rows", [HEADS, CHUNK])
        turns = sb("turns", [P, CHUNK])
        z = sb("z", [P, TILES, NE])
        ez = sb("ez", [P, TILES, NE])
        prob = sb("prob", [P, TILES, 2 * NE])
        rest = sb("rest", [P, TILES, 2 * NE])
        best = sb("best", [P, TILES, 8])
        keys = sb("keys", [P, TILES, 8])
        cand = sb("cand", [P, TILES, NE])
        cw = sb("cw", [P, TILES, NE])
        top = sb("top", [P, 8, TILES])
        cw_rows = sb("cw_rows", [LO + NE, 2 * CHUNK], F32R)
        ff = sb("ff", [P, 2 * CHUNK])
        ff_hi = sb("ff_hi", [P, 2 * CHUNK], F32R)
        ff_lo = sb("ff_lo", [P, 2 * CHUNK], F32R)
        xs = sb("xs", [P, 2, CHUNK])
        xs_hi = sb("xs_hi", [P, 2, CHUNK], F32R)
        xs_lo = sb("xs_lo", [P, 2, CHUNK], F32R)
        sg = sb("sg", [P, 2, CHUNK])
        h = sb("h", [P, 2, CHUNK])
        h_hi = sb("h_hi", [P, 3, CHUNK], F32R)
        h_lo = sb("h_lo", [P, 3, CHUNK], F32R)
        y_t = sb("y_t", [P, CHUNK])
        y_stats = sb("y_stats", [P, TILES, 6])
        y_mom = sb("y_mom", [P, TILES, 2])

        raw_qkv = y_t[:, 0:3 * E].rearrange("p (w e) -> p w e", w=3)
        pick_expert_f = xs[0:LO + NE].rearrange("p a b -> p (a b)").rearrange("p (e m) -> p e m", e=NE)

        gate_ps = [bank("gate_ps0"), bank("gate_ps1")]
        up_ps = [bank("up_ps0"), bank("up_ps1")]
        y_ps = bank("y_ps")
        w_ps = bank("w_ps")
        a_ps = bank("a_ps")
        o_ps = bank("o_ps")
        a_tok = a_ps[:].rearrange("p (i e) -> p i e", e=E)
        w_tok = w_ps[:].rearrange("p (i e) -> p i e", e=E)

        x_in_landed = [sem(f"x_in_landed{c}") for c in range(CHUNKS)]
        attn_w_landed = sem("attn_w_landed")
        small_w_landed = sem("small_w_landed")
        expert_landed = [sem(f"expert_landed{e}") for e in range(NX)]
        out_stored = sem("out_stored")
        pool_const = sem("pool_const")
        consts_made = sem("consts_made")
        stage_cleared = sem("stage_cleared")
        cw_cleared = sem("cw_cleared")
        keys_made = sem("keys_made")
        small_turned = sem("small_turned")
        small_copied = sem("small_copied")
        fg_composed = sem("fg_composed")
        attn_w_hi = sem("attn_w_hi")
        attn_w_ready = sem("attn_w_ready")
        pick_copied = sem("pick_copied")
        expert_hi = sem("expert_hi")
        expert_lo = sem("expert_lo")
        xn_made = sem("xn_made")
        xn_turned = sem("xn_turned")
        xn_hi_made = sem("xn_hi_made")
        xn_lo_made = sem("xn_lo_made")
        qk_projected = sem("qk_projected")
        qk_made = sem("qk_made")
        fg_projected = sem("fg_projected")
        fg_made = sem("fg_made")
        og_made = sem("og_made")
        sq_made = sem("sq_made")
        sq_summed = sem("sq_summed")
        rs_made = sem("rs_made")
        rs_turned = sem("rs_turned")
        rs_copied = sem("rs_copied")
        rs_spread = sem("rs_spread")
        on_made = sem("on_made")
        attn_projected = sem("attn_projected")
        attn_read = sem("attn_read")
        x2n_made = sem("x2n_made")
        x2_turned = sem("x2_turned")
        x2_copied = sem("x2_copied")
        x2_lo_made = sem("x2_lo_made")
        logits_made = sem("logits_made")
        z_made = sem("z_made")
        exp_made = sem("exp_made")
        cw_made = sem("cw_made")
        cw_turned = sem("cw_turned")
        cw_hi_made = sem("cw_hi_made")
        cw_lo_made = sem("cw_lo_made")
        v_spread = sem("v_spread")
        kv_made = sem("kv_made")
        scanned = sem("scanned")
        carried = sem("carried")
        qs_made = sem("qs_made")
        qs_hi_made = sem("qs_hi_made")
        qs_lo_made = sem("qs_lo_made")
        qs_summed = sem("qs_summed")
        cw_spread = sem("cw_spread")
        xs_made = sem("xs_made")
        xs_hi_made = sem("xs_hi_made")
        xs_lo_made = sem("xs_lo_made")
        gate_done = sem("gate_done")
        up_done = sem("up_done")
        silu_done = sem("silu_done")
        h_made = sem("h_made")
        h_hi_made = sem("h_hi_made")
        h_lo_made = sem("h_lo_made")
        down_done = sem("down_done")
        y_copied = sem("y_copied")
        y_turned = sem("y_turned")
        y_read = sem("y_read")
        x_out_made = sem("x_out_made")
        x_chain = sem("x_chain")
        late_chain = sem("late_chain")
        y_chain = sem("y_chain")

        def atleast(eng, s, value):
            if not (isinstance(value, int) and value <= 0):
                eng.wait_ge(s, value)

        def cols(c):
            return bass.ds(c * CHUNK, CHUNK)

        def ff_cols(c):
            return bass.ds((c % 2) * CHUNK, CHUNK)

        def tile_of(buf, c, i):
            return buf[:, bass.ds(c * TILES + i, 1), :].squeeze(1)

        def tiles(c):
            return bass.ds(c * TILES, TILES)

        def three(out_ap, w_hi, w_lo, v_hi, v_lo, start=True, stop=True):
            nc.tensor.matmul(out_ap, w_hi, v_hi, start=start, stop=False)
            nc.tensor.matmul(out_ap, w_hi, v_lo, start=False, stop=False)
            return nc.tensor.matmul(out_ap, w_lo, v_hi, start=False, stop=stop)

        def round_of(c, feed_forward, late, early, end):
            for slot in range(STEPS):
                n = slot + HEAD
                if n < STEPS:
                    feed_forward(n, c, late is not None)
                else:
                    feed_forward(n - STEPS, c + 1, late is not None)
                for stage in EARLY_AT.get(slot, []) if early else []:
                    early(stage, c + 2)
                for stage in LATE_AT.get(slot, []) if late else []:
                    late(stage, c + 1)
                for stage in END_AT.get(slot, []):
                    end(stage, c)

        def program(eng, feed_forward, late, early, end, expert=None, late_counted=None):
            split = 0
            for stage in EARLY:
                early(stage, 0)
                if expert and stage in (1, 3, 11, 12):
                    expert(split)
                    split += 1
            for stage in EARLY:
                if stage + LATE[0] in LATE:
                    late(stage + LATE[0], 0)
                early(stage, 1)
                if expert and stage % 2 == 1 and split < NX:
                    expert(split)
                    split += 1
            if late_counted:
                late_counted()
            for n in range(HEAD):
                feed_forward(n, 0, False)
            with eng.Fori(0, CHUNKS - 2) as c:
                round_of(c, feed_forward, late, early, end)
            round_of(CHUNKS - 2, feed_forward, late, None, end)
            for n in range(HEAD, STEPS):
                feed_forward(n, CHUNKS - 1, False)
            for n in range(2):
                feed_forward(n, CHUNKS, False)
            for stage in range(4):
                end(stage, CHUNKS - 1)

        def spread_bank(c, v):
            return gate_ps[0] if isinstance(c, int) and c < 2 and v % 2 else a_ps

        block = ctx.enter_context(nc.Block())

        @block.sync
        def _(sp):
            def load_expert(n):
                landed = expert_landed[n]
                gate, up, down = ((sw_gate, sw_up, sw_down) if n == 0
                                  else (we_gate[n - 1], we_up[n - 1], we_down[n - 1]))
                s = n % STAGE
                if n >= STAGE:
                    sp.wait_ge(expert_lo, n - STAGE + 1)
                sp.dma_start(raw_gu[:, s, 0, :], gate).then_inc(landed, 16)
                sp.dma_start(raw_gu[:, s, 1, :], up).then_inc(landed, 16)
                if n == 0:
                    sp.wait_ge(stage_cleared, 1)
                whole = FD // P * P
                sp.dma_start(raw_down[:, s, 0:FD // P, :],
                             down[0:whole, :].rearrange("(j p) e -> p j e", p=P)).then_inc(landed, 16)
                sp.dma_start(raw_down[0:FD - whole, s, FD // P, :], down[whole:FD, :]).then_inc(landed, 16)

            x_tok = x[0].rearrange("(i p) e -> p i e", p=P)
            sp.dma_start(x_res[:, 0:TILES, :], x_tok[:, 0:TILES, :]).then_inc(x_in_landed[0], 16)
            for i, w in enumerate((Wq, Wk, Wv)):
                sp.dma_start(raw_qkv[:, i, :], w).then_inc(attn_w_landed, 16)
            load_expert(0)
            for c in range(1, CHUNKS):
                sp.dma_start(x_res[:, c * TILES:(c + 1) * TILES, :],
                             x_tok[:, c * TILES:(c + 1) * TILES, :]).then_inc(x_in_landed[c], 16)
            for n in range(1, NX):
                load_expert(n)
            out_tok = out[0].rearrange("(i p) e -> p i e", p=P)
            with sp.Fori(0, CHUNKS) as c:
                sp.wait_ge(x_out_made, c + 1)
                sp.dma_start(out_tok[:, tiles(c), :], x_res[:, tiles(c), :]).then_inc(out_stored, 16)
            sp.wait_ge(out_stored, 16 * CHUNKS)

        @block.gpsimd
        def _(pool):
            nc.gpsimd.memset(ident[:], 0.0)
            nc.gpsimd.memset(head_of[:], 1.0)
            nc.gpsimd.memset(head_rows[:], 1.0)
            nc.gpsimd.memset(pick_expert_f, 0.0).then_inc(pool_const, 1)
            pool.wait_ge(pool_const, 1)
            nc.gpsimd.affine_select(out=ident[:], in_=ident[:], compare_op=ALU.not_equal, fill=1.0,
                                    base=0, pattern=[[-1, P]], channel_multiplier=1)
            nc.gpsimd.affine_select(out=head_of[:], in_=head_of[:], compare_op=ALU.is_ge, fill=0.0,
                                    base=0, pattern=[[-D, HEADS]], channel_multiplier=1)
            nc.gpsimd.affine_select(out=head_rows[:], in_=head_rows[:], compare_op=ALU.is_ge, fill=0.0,
                                    base=0, pattern=[[1, P]], channel_multiplier=-D)
            nc.gpsimd.affine_select(out=pick_expert_f, in_=pick_expert_f, compare_op=ALU.not_equal,
                                    fill=1.0, base=0, pattern=[[-1, NE], [0, P]],
                                    channel_multiplier=1).then_inc(pool_const, 1)
            pool.wait_ge(pool_const, 2)
            nc.gpsimd.affine_select(out=head_of[:], in_=head_of[:], compare_op=ALU.is_ge, fill=0.0,
                                    base=D - 1, pattern=[[D, HEADS]], channel_multiplier=-1)
            nc.gpsimd.affine_select(out=head_rows[:], in_=head_rows[:], compare_op=ALU.is_ge, fill=0.0,
                                    base=D - 1, pattern=[[-1, P]], channel_multiplier=D)
            nc.gpsimd.affine_select(out=pick_expert_f, in_=pick_expert_f, compare_op=ALU.not_equal,
                                    fill=1.0, base=-LO, pattern=[[-1, NE], [0, P]],
                                    channel_multiplier=1).then_inc(consts_made, 1)
            nc.gpsimd.memset(raw_down[:], 0.0).then_inc(stage_cleared, 1)
            nc.gpsimd.memset(cw_rows[:].bitcast(F32), 0.0).then_inc(cw_cleared, 1)
            nc.gpsimd.memset(prob[:, :, NE:2 * NE], -1.0)
            nc.gpsimd.memset(keys[:], -1.0).then_inc(keys_made, 1)

            def early(s, c):
                if 5 <= s < 5 + D:
                    v = s - 5
                    pool.wait_ge(scanned, D * c + v + 1)
                    pool.nop(nofuse=True)
                    nc.gpsimd.tensor_copy(carry[:, v:v + 1], state[:, v % 2, CHUNK - 1:CHUNK]).then_inc(carried, 1)
                    pool.wait_ge(qs_hi_made, D * c + v + 1)
                    nc.gpsimd.tensor_tensor(qs_lo[:, v % 2, :], qs[:, v % 2, :], qs_hi[:, v % 2, :].bitcast(F32),
                                            ALU.subtract).then_inc(qs_lo_made, 1)

            def late(s, c):
                pass

            def end(s, c):
                pass

            def feed_forward(n, c, beside):
                if isinstance(c, int) and c == CHUNKS and n == 1:
                    return
                if n >= 1 or not (isinstance(c, int) and c == 0):
                    before = (n - 1) % STEPS
                    pool.wait_ge(h_hi_made, STEPS * c + n)
                    nc.gpsimd.tensor_tensor(h_lo[:, before % 3, :], h[:, before % 2, :],
                                            h_hi[:, before % 3, :].bitcast(F32),
                                            ALU.subtract).then_inc(h_lo_made, 1)
                e, j = divmod(n, NJ)
                if j == 1 and e < NE and not (isinstance(c, int) and c == CHUNKS):
                    pool.wait_ge(xs_hi_made, NE * c + e + 1)
                    nc.gpsimd.tensor_tensor(xs_lo[:, e % 2, :], xs[:, e % 2, :], xs_hi[:, e % 2, :].bitcast(F32),
                                            ALU.subtract).then_inc(xs_lo_made, 1)

            def expert(n):
                pool.wait_ge(expert_hi, n + 1)
                s = n % STAGE
                nc.gpsimd.tensor_tensor(gu_lo[:, n], raw_gu[:, s], gu_hi[:, n].bitcast(F32), ALU.subtract)
                nc.gpsimd.tensor_tensor(down_lo[:, n], raw_down[:, s], down_hi[:, n].bitcast(F32),
                                        ALU.subtract).then_inc(expert_lo, 1)

            program(pool, feed_forward, late, early, end, expert)

        @block.scalar
        def _(act):
            act.dma_start(raw_fg1[:, 0, :], Wf1).then_inc(small_w_landed, 16)
            act.dma_start(raw_fg1[:, 1, :], Wg1).then_inc(small_w_landed, 16)
            act.dma_start(raw_fg2[:, 0, :], Wf2).then_inc(small_w_landed, 16)
            act.dma_start(raw_fg2[:, 1, :], Wg2).then_inc(small_w_landed, 16)
            act.dma_start(raw_route[:], gate_w).then_inc(small_w_landed, 16)
            act.dma_start(norm_w[:], norm_weight.rearrange("(p a) -> p a", a=1)).then_inc(small_w_landed, 16)
            act.dma_start(w_out[:], Wo).then_inc(small_w_landed, 16)

            def copy(dst, src):
                return nc.scalar.activation(dst, src, ACT.Copy)

            def early(s, c):
                if s == 1:
                    act.wait_ge(xn_turned, c + 1)
                    atleast(act, v_spread, D * c)
                    copy(xn_hi[:], a_ps[:]).then_inc(xn_hi_made, 1)
                if s == 2:
                    act.wait_ge(qk_projected, c + 1)
                    atleast(act, qs_made, D * c)
                    nc.scalar.activation(q[:], a_ps[:], ACT.Silu)
                    nc.scalar.activation(k[:], o_ps[:], ACT.Silu).then_inc(qk_made, 1)
                if s == 3:
                    act.wait_ge(fg_projected, c + 1)
                    atleast(act, og_made, c)
                    nc.scalar.activation(f[:], a_ps[:], ACT.Sigmoid)
                    nc.scalar.activation(g[:], o_ps[:], ACT.Sigmoid).then_inc(fg_made, 1)
                if 5 <= s < 5 + D:
                    v = s - 5
                    act.wait_ge(qs_made, D * c + v + 1)
                    atleast(act, qs_summed, D * c + v - 1)
                    copy(qs_hi[:, v % 2, :], qs[:, v % 2, :]).then_inc(qs_hi_made, 1)

            def late(s, c):
                if s == 14:
                    act.wait_ge(og_made, c + 1)
                    atleast(act, logits_made, c)
                    nc.scalar.activation(turns[:], og[:], ACT.Square).then_inc(sq_made, 1)
                if s == 15:
                    act.wait_ge(rs_turned, c + 1)
                    atleast(act, rs_spread, c)
                    copy(rs_rows[:], w_ps[0:HEADS, :]).then_inc(rs_copied, 1)
                if s == 21:
                    act.wait_ge(x2_turned, c + 1)
                    half = ff_cols(c)
                    copy(turns[:], w_ps[:])
                    copy(ff[:, half], w_ps[:])
                    copy(ff_hi[:, half], w_ps[:]).then_inc(x2_copied, 1)
                if s == 23:
                    act.wait_ge(z_made, c + 1)
                    nc.scalar.activation(ez[:], z[:], ACT.Exp).then_inc(exp_made, 1)
                if s == 25:
                    act.wait_ge(cw_turned, c + 1)
                    if isinstance(c, int):
                        act.wait_ge(cw_cleared, 1)
                    copy(cw_rows[0:NE, ff_cols(c)], w_ps[0:NE, :]).then_inc(cw_hi_made, 1)

            def feed_forward(n, c, beside):
                if not (isinstance(c, int) and c == CHUNKS):
                    act.wait_ge(gate_done, STEPS * c + n + 1)
                    atleast(act, h_made, STEPS * c + max(n - 1, 0))
                    r = ROWS[n % NJ][1]
                    nc.scalar.activation(sg[0:r, n % 2, :], gate_ps[n % 2][0:r, :], ACT.Silu).then_inc(silu_done, 1)
                elif n == 1:
                    return
                if n >= 1 or not (isinstance(c, int) and c == 0):
                    before = (n - 1) % STEPS
                    act.wait_ge(h_made, STEPS * c + n)
                    atleast(act, down_done, STEPS * c + n - 3)
                    copy(h_hi[:, before % 3, :], h[:, before % 2, :]).then_inc(h_hi_made, 1)
                e, j = divmod(n, NJ)
                if j == 1 and e < NE:
                    act.wait_ge(xs_made, NE * c + e + 1)
                    atleast(act, up_done, STEPS * c + (NJ * e if e >= 2 else 0))
                    copy(xs_hi[:, e % 2, :], xs[:, e % 2, :]).then_inc(xs_hi_made, 1)

            def end(s, c):
                if s == 0:
                    act.wait_ge(down_done, STEPS * (c + 1))
                    copy(y_t[:], y_ps[:]).then_inc(y_copied, 1)

            def expert(n):
                act.wait_ge(expert_landed[n], 64)
                if n == 0:
                    act.wait_ge(stage_cleared, 1)
                s = n % STAGE
                copy(gu_hi[:, n], raw_gu[:, s])
                copy(down_hi[:, n], raw_down[:, s]).then_inc(expert_hi, 1)

            program(act, feed_forward, late, early, end, expert)

        @block.vector
        def _(dve):
            Y_LINKS = 3 + 1 + 3 * NEWTON_STEPS + 1
            per_chunk = {y_chain: Y_LINKS}
            done = {}

            def link(chain, c, ins):
                done[chain] = done.get(chain, 0) + 1
                ins.then_inc(chain, 1)
                dve.wait_ge(chain, c * per_chunk.get(chain, 0) + done[chain])

            def rsqrt(chain, c, out_ap, n):
                v, y, t, mh = var_eps[:, 0:n], out_ap, newton[:, 0:n], minus_half[:, 0:n]
                nc.vector.tensor_scalar(mh, v, -0.5, None, ALU.mult)
                link(chain, c, nc.vector.tensor_scalar(y.bitcast(I32), v.bitcast(I32), -0.5, float(RSQRT_MAGIC),
                                                       ALU.mult, ALU.add))
                for step in range(NEWTON_STEPS):
                    link(chain, c, nc.vector.tensor_tensor(t, y, y, ALU.mult))
                    link(chain, c, nc.vector.tensor_tensor(t, t, mh, ALU.mult))
                    last = nc.vector.scalar_tensor_tensor(y, t, 1.5, y, ALU.add, ALU.mult)
                    if step < NEWTON_STEPS - 1:
                        link(chain, c, last)
                return last

            def tile_stats(chain, c, src, mom, count=TILES):
                for i in range(count):
                    last = nc.vector.bn_stats(stats[:, i, :], src(i))
                link(chain, c, last)
                dve.nop(nofuse=True)
                for i in range(count):
                    last = nc.vector.bn_aggr(mom[:, i, :], stats[:, i, :])
                link(chain, c, last)
                link(chain, c, nc.vector.tensor_scalar(var_eps[:, 0:count], mom[:, 0:count, 1], EPS, None,
                                                       ALU.add))

            def normalise(dst, src, mean, rstd):
                for i in range(TILES):
                    last = nc.vector.tensor_scalar(dst[:, i, :], src(i), mean(i), rstd(i),
                                                   ALU.subtract, ALU.mult)
                return last

            def mean(i):
                return moments[:, i, 0:1]

            def rstd(i):
                return rs[:, i:i + 1]

            def spread(ap):
                return ap.unsqueeze(2).to_broadcast([P, TILES, NE])

            def early(s, c):
                if s == 0:
                    if isinstance(c, int) and c < 2:
                        at, count = (0, TILES) if c == 0 else (TILES, TOKENS // P - TILES)
                        for landed in x_in_landed[0:1] if c == 0 else x_in_landed[1:]:
                            dve.wait_ge(landed, 16)
                        tile_stats(x_chain, 0, lambda i: x_res[:, at + i, :], x_mom[:, at:at + count, :], count)
                        link(x_chain, 0, rsqrt(x_chain, 0, x_rs[:, at:at + count], count))
                    atleast(dve, xn_turned, c)
                    normalise(xn, lambda i: tile_of(x_res, c, i),
                              lambda i: x_mom[:, bass.ds(c * TILES + i, 1), 0:1].squeeze(1),
                              lambda i: x_rs[:, bass.ds(c * TILES + i, 1)]).then_inc(xn_made, 1)
                if s == 1:
                    dve.wait_ge(xn_hi_made, c + 1)
                    nc.vector.tensor_tensor(xn_lo[:], a_ps[:], xn_hi[:].bitcast(F32),
                                            ALU.subtract).then_inc(xn_lo_made, 1)
                if 4 <= s < 4 + D:
                    v = s - 4
                    if v == 0:
                        dve.wait_ge(qk_made, c + 1)
                        dve.wait_ge(fg_made, c + 1)
                    dve.wait_ge(v_spread, D * c + v + 1)
                    kv = spread_bank(c, v)
                    nc.vector.tensor_tensor(kv[:], kv[:], k[:], ALU.mult).then_inc(kv_made, 1)
                    dve.wait_ge(kv_made, D * c + v + 1)
                    atleast(dve, carried, D * c + v - 1)
                    first_state = 0.0 if isinstance(c, int) and c == 0 else carry[:, v:v + 1]
                    nc.vector.tensor_tensor_scan(state[:, v % 2, :], f[:], kv[:], first_state,
                                                 ALU.mult, ALU.add).then_inc(scanned, 1)
                    dve.wait_ge(scanned, D * c + v + 1)
                    atleast(dve, qs_lo_made, D * c + v - 1)
                    nc.vector.tensor_tensor(qs[:, v % 2, :], state[:, v % 2, :], q[:], ALU.mult).then_inc(qs_made, 1)
                if s == 13:
                    dve.wait_ge(qs_summed, D * c + D)
                    nc.vector.scalar_tensor_tensor(og[:], o_ps[:], SCALE, g[:], ALU.mult,
                                                   ALU.mult).then_inc(og_made, 1)

            def late(s, c):
                def lk(ins):
                    link(late_chain, c, ins)

                if s == 14:
                    dve.wait_ge(sq_summed, c + 1)
                    done[late_chain] = 0
                    lk(nc.vector.tensor_scalar(var_eps[:], w_ps[:, 0:TILES * HEADS], 1.0 / D, EPS,
                                               ALU.mult, ALU.add))
                    rsqrt(late_chain, c, rs[:], TILES * HEADS).then_inc(rs_made, 1)
                if s == 16:
                    dve.wait_ge(rs_spread, c + 1)
                    nc.vector.scalar_tensor_tensor(turns[:], og[:], norm_w[:], w_ps[:], ALU.mult,
                                                   ALU.mult).then_inc(on_made, 1)
                if s == 17:
                    dve.wait_ge(attn_projected, c + 1)
                    tile_stats(late_chain, c, lambda i: w_tok[:, i, :], moments)
                if s == 18:
                    lk(rsqrt(late_chain, c, rs[:, 0:TILES], TILES))
                    normalise(an, lambda i: w_tok[:, i, :], mean, rstd).then_inc(attn_read, 1)
                    dve.wait_ge(attn_read, c + 1)
                    lk(nc.vector.tensor_tensor(x_res[:, tiles(c), :], an[:], x_res[:, tiles(c), :],
                                               ALU.add))
                if s == 19:
                    tile_stats(late_chain, c, lambda i: tile_of(x_res, c, i), moments)
                if s == 20:
                    lk(rsqrt(late_chain, c, rs[:, 0:TILES], TILES))
                    normalise(an, lambda i: tile_of(x_res, c, i), mean, rstd).then_inc(x2n_made, 1)
                if s == 21:
                    dve.wait_ge(x2_copied, c + 1)
                    half = ff_cols(c)
                    nc.vector.tensor_tensor(ff_lo[:, half], w_ps[:], ff_hi[:, half].bitcast(F32),
                                            ALU.subtract).then_inc(x2_lo_made, 1)
                if s == 22:
                    dve.wait_ge(logits_made, c + 1)
                    logits = w_ps[:, 0:TILES * NE].rearrange("p (i e) -> p i e", e=NE)
                    lk(nc.vector.tensor_reduce(top[:, 0, :], logits, AX_X, ALU.max))
                    nc.vector.tensor_tensor(z[:], logits, spread(top[:, 0, :]), ALU.subtract).then_inc(z_made, 1)
                if s == 23:
                    dve.wait_ge(exp_made, c + 1)
                    lk(nc.vector.tensor_reduce(top[:, 1, :], ez[:], AX_X, ALU.add))
                    lk(nc.vector.reciprocal(top[:, 2, :], top[:, 1, :]))
                    lk(nc.vector.tensor_tensor(prob[:, :, 0:NE], ez[:], spread(top[:, 2, :]), ALU.mult))
                    dve.nop(nofuse=True)
                    for i in range(TILES):
                        last = nc.vector.max(best[:, i, :], prob[:, i, 0:NE])
                    lk(last)
                    nc.vector.tensor_copy(keys[:, :, 0:2], best[:, :, 0:2])
                    lk(nc.vector.tensor_tensor(top[:, 3, :], best[:, :, 0], best[:, :, 1], ALU.add))
                if s == 24:
                    for i in range(TILES):
                        nc.vector.match_replace(rest[:, i, :], keys[:, i, :], prob[:, i, :], 0.0)
                    lk(nc.vector.tensor_scalar(top[:, 4, :], top[:, 3, :], 1e-20, None, ALU.add))
                    nc.vector.tensor_tensor(cand[:], prob[:, :, 0:NE], rest[:, :, 0:NE], ALU.subtract)
                    lk(nc.vector.reciprocal(top[:, 5, :], top[:, 4, :]))
                    nc.vector.tensor_tensor(cw[:], cand[:], spread(top[:, 5, :]), ALU.mult).then_inc(cw_made, 1)
                if s == 25:
                    dve.wait_ge(cw_hi_made, c + 1)
                    nc.vector.tensor_tensor(cw_rows[LO:LO + NE, ff_cols(c)], w_ps[0:NE, :],
                                            cw_rows[0:NE, ff_cols(c)].bitcast(F32),
                                            ALU.subtract).then_inc(cw_lo_made, 1)

            def feed_forward(n, c, beside):
                if isinstance(c, int) and c == CHUNKS:
                    return
                r = ROWS[n % NJ][1]
                dve.wait_ge(silu_done, STEPS * c + n + 1)
                dve.wait_ge(up_done, STEPS * c + n + 1)
                atleast(dve, h_lo_made, STEPS * c + max(n - 1, 0))
                nc.vector.tensor_tensor(h[0:r, n % 2, :], sg[0:r, n % 2, :], up_ps[n % 2][0:r, :],
                                        ALU.mult).then_inc(h_made, 1)
                e, j = divmod(n, NJ)
                if j == 0 and e < NE:
                    dve.wait_ge(cw_spread, NE * c + e + 1)
                    atleast(dve, xs_lo_made, NE * c + e - 1)
                    nc.vector.tensor_tensor(xs[:, e % 2, :], ff[:, ff_cols(c)], w_ps[:],
                                            ALU.mult).then_inc(xs_made, 1)

            def end(s, c):
                if s == 1:
                    dve.wait_ge(y_turned, c + 1)
                    done[y_chain] = 0
                    tile_stats(y_chain, c, lambda i: a_tok[:, i, :], moments)
                if s == 2:
                    link(y_chain, c, rsqrt(y_chain, c, rs[:, 0:TILES], TILES))
                if s == 3:
                    link(y_chain, c, normalise(an, lambda i: a_tok[:, i, :], mean, rstd))
                    nc.vector.tensor_tensor(x_res[:, tiles(c), :], an[:], x_res[:, tiles(c), :],
                                            ALU.add).then_inc(x_out_made, 1)

            def late_counted():
                per_chunk[late_chain] = done[late_chain]

            dve.wait_ge(attn_w_landed, 48)
            v_cols = raw_qkv[:, 2, :].rearrange("p (h v) -> p v h", v=D).unsqueeze(3).to_broadcast([P, D, HEADS, D])
            vh = vrep_hi[:].rearrange("p v (h k) -> p v h k", k=D)
            vl = vrep_lo[:].rearrange("p v (h k) -> p v h k", k=D)
            nc.vector.tensor_copy(proj_hi[:, 0:2, :], raw_qkv[:, 0:2, :])
            nc.vector.tensor_copy(vh, v_cols).then_inc(attn_w_hi, 1)
            dve.wait_ge(attn_w_hi, 1)
            nc.vector.tensor_tensor(proj_lo[:, 0:2, :], raw_qkv[:, 0:2, :], proj_hi[:, 0:2, :].bitcast(F32),
                                    ALU.subtract)
            nc.vector.tensor_tensor(vl, v_cols, vh.bitcast(F32), ALU.subtract).then_inc(attn_w_ready, 1)
            dve.wait_ge(small_turned, 1)
            nc.vector.tensor_copy(fg1_t[:], a_ps[0:D, 0:2 * E].rearrange("d (g e) -> d g e", g=2))
            nc.vector.tensor_copy(route_t[:], a_ps[:, 2 * E:2 * E + NE]).then_inc(small_copied, 1)
            dve.wait_ge(fg_composed, 1)
            fg = o_ps[:, 0:2 * E].rearrange("p (g e) -> p g e", g=2)
            nc.vector.tensor_copy(proj_hi[:, 2:4, :], fg).then_inc(attn_w_hi, 1)
            dve.wait_ge(attn_w_hi, 2)
            nc.vector.tensor_tensor(proj_lo[:, 2:4, :], fg, proj_hi[:, 2:4, :].bitcast(F32),
                                    ALU.subtract).then_inc(attn_w_ready, 1)
            nc.vector.memset(pick_v[:].bitcast(F32), 0.0).then_inc(pick_copied, 1)
            dve.wait_ge(pick_copied, 1)
            dve.wait_ge(consts_made, 1)
            for v in range(D):
                nc.vector.tensor_copy(pick_v[:, v, :].rearrange("p (h w) -> p h w", w=D)[:, :, v], head_of[:])
            nc.vector.tensor_copy(pick_expert[:], pick_expert_f).then_inc(pick_copied, 1)
            dve.wait_ge(keys_made, 1)

            program(dve, feed_forward, late, early, end, None, late_counted)

        @block.tensor
        def _(pe):
            def turn(dst, src, rows=P):
                return nc.tensor.transpose(dst, src, ident[0:rows, 0:rows])

            def early(s, c):
                if s == 1:
                    pe.wait_ge(xn_made, c + 1)
                    atleast(pe, scanned, D * c)
                    for i in range(TILES):
                        last = turn(a_tok[:, i, :], xn[:, i, :])
                    last.then_inc(xn_turned, 1)
                if s == 2:
                    pe.wait_ge(xn_lo_made, c + 1)
                    if isinstance(c, int):
                        pe.wait_ge(attn_w_ready, 1)
                    three(a_ps[:], proj_hi[:, 0, :], proj_lo[:, 0, :], xn_hi[:], xn_lo[:])
                    atleast(pe, og_made, c)
                    three(o_ps[:], proj_hi[:, 1, :], proj_lo[:, 1, :], xn_hi[:], xn_lo[:]).then_inc(qk_projected, 1)
                if s == 3:
                    if isinstance(c, int):
                        pe.wait_ge(attn_w_ready, 2)
                    pe.wait_ge(qk_made, c + 1)
                    three(a_ps[:], proj_hi[:, 2, :], proj_lo[:, 2, :], xn_hi[:], xn_lo[:])
                    three(o_ps[:], proj_hi[:, 3, :], proj_lo[:, 3, :], xn_hi[:], xn_lo[:]).then_inc(fg_projected, 1)
                if 4 <= s < 4 + D:
                    v = s - 4
                    if v == 0:
                        pe.wait_ge(fg_made, c + 1)
                    ring = 2 if isinstance(c, int) and c < 2 else 1
                    atleast(pe, scanned, D * c + max(v + 1 - ring, 0))
                    three(spread_bank(c, v)[:], vrep_hi[:, v, :], vrep_lo[:, v, :], xn_hi[:],
                          xn_lo[:]).then_inc(v_spread, 1)
                if 6 <= s < 6 + D:
                    v = s - 6
                    if v == 0 and isinstance(c, int):
                        pe.wait_ge(pick_copied, 2)
                    pe.wait_ge(qs_lo_made, D * c + v + 1)
                    nc.tensor.matmul(o_ps[:], pick_v[:, v, :], qs_hi[:, v % 2, :], start=(v == 0), stop=False)
                    nc.tensor.matmul(o_ps[:], pick_v[:, v, :], qs_lo[:, v % 2, :], start=False,
                                     stop=(v == D - 1)).then_inc(qs_summed, 1)

            def late(s, c):
                def xs_read():
                    if not (isinstance(c, int) and c == 0):
                        pe.wait_ge(xs_made, NE * (c - 1) + min(LATE_STEP[s] // NJ + 1, NE))

                if s == 14:
                    pe.wait_ge(sq_made, c + 1)
                    xs_read()
                    for i in range(TILES):
                        last = nc.tensor.matmul(w_ps[:, i * HEADS:(i + 1) * HEADS], turns[:, i * P:(i + 1) * P],
                                                head_of[:], start=True, stop=True)
                    last.then_inc(sq_summed, 1)
                if s == 15:
                    pe.wait_ge(rs_made, c + 1)
                    for i in range(TILES):
                        last = turn(w_ps[0:HEADS, i * P:(i + 1) * P], rs[:, i * HEADS:(i + 1) * HEADS])
                    last.then_inc(rs_turned, 1)
                if s == 16:
                    pe.wait_ge(rs_copied, c + 1)
                    xs_read()
                    nc.tensor.matmul(w_ps[:], head_rows[:], rs_rows[:], start=True, stop=True).then_inc(rs_spread, 1)
                if s == 17:
                    pe.wait_ge(on_made, c + 1)
                    xs_read()
                    for i in range(TILES):
                        last = nc.tensor.matmul(w_tok[:, i, :], turns[:, i * P:(i + 1) * P], w_out[:],
                                                start=True, stop=True)
                    last.then_inc(attn_projected, 1)
                if s == 21:
                    pe.wait_ge(x2n_made, c + 1)
                    xs_read()
                    for i in range(TILES):
                        last = turn(w_tok[:, i, :], an[:, i, :])
                    last.then_inc(x2_turned, 1)
                if s == 22:
                    pe.wait_ge(x2_lo_made, c + 1)
                    xs_read()
                    for i in range(TILES):
                        last = nc.tensor.matmul(w_ps[:, i * NE:(i + 1) * NE], turns[:, i * P:(i + 1) * P],
                                                route_t[:], start=True, stop=True)
                    last.then_inc(logits_made, 1)
                if s == 25:
                    pe.wait_ge(cw_made, c + 1)
                    xs_read()
                    for i in range(TILES):
                        last = turn(w_ps[0:NE, i * P:(i + 1) * P], cw[:, i, :])
                    last.then_inc(cw_turned, 1)

            def down(n, c):
                r = ROWS[n % NJ][1]
                e, j = divmod(n, NJ)
                pe.wait_ge(h_lo_made, STEPS * c + n + 1)
                if n == 0:
                    atleast(pe, y_copied, c)
                three(y_ps[:], down_hi[0:r, e, j, :], down_lo[0:r, e, j, :], h_hi[0:r, n % 3, :],
                      h_lo[0:r, n % 3, :], start=(n == 0), stop=(n == STEPS - 1)).then_inc(down_done, 1)

            bank_left = {3: on_made, 4: attn_read, 6: z_made}

            def feed_forward(n, c, beside):
                if isinstance(c, int) and c == CHUNKS:
                    down(STEPS - 2 + n, c - 1)
                    return
                e, j = divmod(n, NJ)
                row, r = ROWS[j]
                half = ff_cols(c)
                x_hi, x_lo = ff_hi[:, half], ff_lo[:, half]
                if n == 0:
                    pe.wait_ge(x2_lo_made, c + 1)
                    pe.wait_ge(cw_lo_made, c + 1)
                if j == 0 and isinstance(c, int) and c == 0 or n >= HEAD and j == 0:
                    pe.wait_ge(expert_lo, e + 1)
                if j == 0 and e < NE:
                    if e >= 1:
                        pe.wait_ge(xs_made, NE * c + e)
                    if beside and e in bank_left:
                        pe.wait_ge(bank_left[e], c + 2)
                    pe.nop(nofuse=True)
                    nc.tensor.matmul(w_ps[:], pick_expert[:, e, :], cw_rows[:, half],
                                     start=True, stop=True).then_inc(cw_spread, 1)
                atleast(pe, silu_done, STEPS * c + max(n - 1, 0))
                three(gate_ps[n % 2][0:r, :], gu_hi[:, e, 0, row:row + r], gu_lo[:, e, 0, row:row + r],
                      x_hi, x_lo).then_inc(gate_done, 1)
                if e >= 1:
                    pe.wait_ge(xs_lo_made, NE * c + e)
                    u_hi, u_lo = xs_hi[:, (e - 1) % 2, :], xs_lo[:, (e - 1) % 2, :]
                else:
                    u_hi, u_lo = x_hi, x_lo
                atleast(pe, h_made, STEPS * c + max(n - 1, 0))
                three(up_ps[n % 2][0:r, :], gu_hi[:, e, 1, row:row + r], gu_lo[:, e, 1, row:row + r],
                      u_hi, u_lo).then_inc(up_done, 1)
                if n >= 2:
                    down(n - 2, c)
                elif not (isinstance(c, int) and c == 0):
                    down(STEPS - 2 + n, c - 1)

            def end(s, c):
                if s == 1:
                    pe.wait_ge(y_copied, c + 1)
                    pe.wait_ge(scanned, D * min(c + 3, CHUNKS) if isinstance(c, int) else D * (c + 3))
                    for i in range(TILES):
                        last = turn(a_tok[:, i, :], y_t[:, i * P:(i + 1) * P])
                    last.then_inc(y_turned, 1)

            pe.wait_ge(small_w_landed, 16 * 7)
            pe.wait_ge(consts_made, 1)
            for i in range(2):
                turn(a_ps[0:D, i * E:(i + 1) * E], raw_fg1[:, i, :])
            turn(a_ps[:, 2 * E:2 * E + NE], raw_route[:], NE).then_inc(small_turned, 1)
            pe.wait_ge(small_copied, 1)
            for i in range(2):
                last = nc.tensor.matmul(o_ps[:, i * E:(i + 1) * E], fg1_t[:, i, :], raw_fg2[:, i, :],
                                        start=True, stop=True)
            last.then_inc(fg_composed, 1)

            program(pe, feed_forward, late, early, end)


_INS = ["x", "Wq", "Wk", "Wv", "Wo", "Wf1", "Wf2", "Wg1", "Wg2", "norm_weight"]
_FFN = ["gate_w", "we_gate", "we_up", "we_down", "sw_gate", "sw_up", "sw_down"]


def kernel(**inputs):
    import numpy as np
    import concourse.bacc as bacc
    from concourse.bass_utils import run_bass_kernel_spmd

    nc = bacc.Bacc("TRN2", target_bir_lowering=False, num_devices=1)
    arrays, args = {}, []
    for name in ["L0_attn_" + n for n in _INS] + ["L0_ffn_" + n for n in _FFN]:
        a = np.ascontiguousarray(inputs[name])
        arrays[f"in_{name}"] = a
        args.append(nc.dram_tensor(f"in_{name}", a.shape, mybir.dt.from_np(a.dtype), kind="ExternalInput").ap())
    shape = inputs["L0_attn_x"].shape
    out = nc.dram_tensor("out_0", shape, F32, kind="ExternalOutput").ap()
    build(nc, *args, out)
    r = run_bass_kernel_spmd(nc, [arrays], core_ids=[0])
    return r.results[0]["out_0"]
```

```python
from contextlib import ExitStack

import concourse.bass as bass
from concourse import mybir

P = 128
F32 = mybir.dt.float32
F32R = mybir.dt.float32r
I32 = mybir.dt.int32
ALU = mybir.AluOpType
ACT = mybir.ActivationFunctionType
AX_X = mybir.AxisListType.X

CHUNK = 512
TILES = CHUNK // P
EPS = 1e-5
RSQRT_MAGIC = 0x5F3759DF
NEWTON_STEPS = 3
H_RING = 4


def build(nc, x, Wq, Wk, Wv, Wo, Wf1, Wf2, Wg1, Wg2, norm_weight, gate_w,
          we_gate, we_up, we_down, sw_gate, sw_up, sw_down, out):
    _, TOKENS, E = x.shape
    D = Wf1.shape[1]
    HEADS = E // D
    NE, _, FD = we_gate.shape
    NX = NE + 1
    CHUNKS = TOKENS // CHUNK
    SCALE = float(D) ** -0.5
    ROWS = [(j, min(P, FD - j)) for j in range(0, FD, P)]
    NJ = len(ROWS)
    STEPS = NX * NJ
    LO = 32
    LAG = H_RING - 1
    STAGE = 2
    HEAD = 5
    EARLY_AT = {0: [0], 1: [1], 2: [2], 3: [3], 4: [4], 5: [5], 7: [6], 8: [7], 13: [8], 16: [9],
                17: [10], 18: [11], 19: [12], 20: [13]}
    LATE_AT = {1: [14], 2: [15, 16], 5: [17], 6: [18], 8: [19], 10: [20], 11: [21], 14: [22],
               15: [23], 16: [24], 18: [25], 19: [26, 27, 28], 21: [29]}
    END_AT = {24: [0, 1], 25: [2], 26: [3]}
    SPLIT_AFTER = (1, 2)
    BESIDE = """X L14 L15 L16 X L17 L18 E0 X L19 X E1 E2 E3 L20 L21 L22 E4 E5 L23 L24 E6 L25 E7 X
        E8 X L26 L27 L28 F0 E9 L29 E10 X F1 E11 F2 E12 E13 F3 F4"""
    ROOMY_V = sum(1 for item in BESIDE.split("F0")[0].split() if item[0] == "E" and 4 <= int(item[1:]) < 4 + D)
    VECTOR_V = (D - 1,)
    EARLY, LATE = range(0, 14), range(14, 30)
    LATE_STEP = {stage: slot + HEAD for slot, stages in LATE_AT.items() for stage in stages}
    assert E == P and TOKENS % CHUNK == 0 and (CHUNKS - 1) * TILES % (D - 2) == 0

    with ExitStack() as ctx:
        def sb(name, shape, dt=F32):
            return ctx.enter_context(nc.sbuf_tensor(name, shape, dt))

        def bank(name):
            return ctx.enter_context(nc.psum_tensor(name, [P, CHUNK], F32))

        def sem(name):
            return ctx.enter_context(nc.semaphore(name))

        w_out = sb("w_out", [P, E])
        raw_fg1 = sb("raw_fg1", [P, 2, D])
        raw_fg2 = sb("raw_fg2", [D, 2, E])
        raw_route = sb("raw_route", [NE, E])
        norm_w = sb("norm_w", [P, 1])
        norm_half = sb("norm_half", [P, 1])
        warm = sb("warm", [1, 1])
        raw_gu = sb("raw_gu", [P, STAGE, 2, FD])
        raw_down = sb("raw_down", [P, STAGE, NJ, E])
        proj_hi = sb("proj_hi", [P, 4, E], F32R)
        proj_lo = sb("proj_lo", [P, 4, E], F32R)
        vrep_hi = sb("vrep_hi", [P, D, E], F32R)
        vrep_lo = sb("vrep_lo", [P, D, E], F32R)
        fg1_t = sb("fg1_t", [D, 2, E])
        route_t = sb("route_t", [P, NE])
        gu_hi = sb("gu_hi", [P, NX, 2, FD], F32R)
        gu_lo = sb("gu_lo", [P, NX, 2, FD], F32R)
        down_hi = sb("down_hi", [P, NX, NJ, E], F32R)
        down_lo = sb("down_lo", [P, NX, NJ, E], F32R)
        ident = sb("ident", [P, P])
        head_of = sb("head_of", [P, HEADS])
        head_rows = sb("head_rows", [HEADS, P])
        pick_v = sb("pick_v", [P, D - 1 + E], F32R)
        pick_expert = sb("pick_expert", [LO + NE, NE, P], F32R)
        x_res = sb("x_res", [P, TOKENS // P, E])
        stats = sb("stats", [P, TOKENS // P, 6])
        x_mom = sb("x_mom", [P, TOKENS // P, 2])
        x_rs = sb("x_rs", [P, TOKENS // P])
        moments = sb("moments", [P, TILES, 2])
        var_eps = sb("var_eps", [P, TILES * HEADS])
        minus_half = sb("minus_half", [P, TILES * HEADS])
        rs = sb("rs", [P, TILES * HEADS])
        newton = sb("newton", [P, TILES * HEADS])
        xn = sb("xn", [P, TILES, E])
        an = sb("an", [P, TILES, E])
        xn_hi = sb("xn_hi", [P, CHUNK], F32R)
        xn_lo = sb("xn_lo", [P, CHUNK], F32R)
        q = sb("q", [P, CHUNK])
        k = sb("k", [P, CHUNK])
        f = sb("f", [P, CHUNK])
        g = sb("g", [P, CHUNK])
        state = sb("state", [P, 2, CHUNK])
        carry = sb("carry", [P, D])
        qs = sb("qs", [P, 2, CHUNK])
        qs_hi = sb("qs_hi", [P, 2, CHUNK], F32R)
        qs_lo = sb("qs_lo", [P, 2, CHUNK], F32R)
        og = sb("og", [P, CHUNK])
        rs_rows = sb("rs_rows", [HEADS, CHUNK])
        turns = sb("turns", [P, CHUNK])
        z = sb("z", [P, TILES, NE])
        ez = sb("ez", [P, TILES, NE])
        prob = sb("prob", [P, TILES, 2 * NE])
        rest = sb("rest", [P, TILES, 2 * NE])
        best = sb("best", [P, TILES, 8])
        keys = sb("keys", [P, TILES, 8])
        cand = sb("cand", [P, TILES, NE])
        cw = sb("cw", [P, TILES, NE])
        top = sb("top", [P, 8, TILES])
        cw_rows = sb("cw_rows", [LO + NE, 2 * CHUNK], F32R)
        ff = sb("ff", [P, 2 * CHUNK])
        ff_hi = sb("ff_hi", [P, 2 * CHUNK], F32R)
        ff_lo = sb("ff_lo", [P, 2 * CHUNK], F32R)
        xs = sb("xs", [P, 2, CHUNK])
        xs_hi = sb("xs_hi", [P, 2, CHUNK], F32R)
        xs_lo = sb("xs_lo", [P, 2, CHUNK], F32R)
        sg = sb("sg", [P, 2, CHUNK])
        h = sb("h", [P, 2, CHUNK])
        h_hi = sb("h_hi", [P, H_RING, CHUNK], F32R)
        h_lo = sb("h_lo", [P, H_RING, CHUNK], F32R)
        y_t = sb("y_t", [P, CHUNK])

        raw_qkv = y_t[:, 0:3 * E].rearrange("p (w e) -> p w e", w=3)
        pick_expert_f = xs[0:LO + NE].rearrange("p a b -> p (a b)").rearrange("p (e m) -> p e m", e=NE)

        gate_ps = [bank("gate_ps0"), bank("gate_ps1")]
        up_ps = [bank("up_ps0"), bank("up_ps1")]
        y_ps = bank("y_ps")
        w_ps = bank("w_ps")
        a_ps = bank("a_ps")
        o_ps = bank("o_ps")
        a_tok = a_ps[:].rearrange("p (i e) -> p i e", e=E)
        w_tok = w_ps[:].rearrange("p (i e) -> p i e", e=E)

        x_in_landed = [sem(f"x_in_landed{c}") for c in range(CHUNKS)]
        attn_w_landed = sem("attn_w_landed")
        gate_w_landed = sem("gate_w_landed")
        small_w_landed = sem("small_w_landed")
        expert_landed = [sem(f"expert_landed{e}") for e in range(NX)]
        out_stored = sem("out_stored")
        pool_const = sem("pool_const")
        consts_made = sem("consts_made")
        stage_cleared = sem("stage_cleared")
        cw_cleared = sem("cw_cleared")
        keys_made = sem("keys_made")
        fg1_turned = sem("fg1_turned")
        fg1_copied = sem("fg1_copied")
        route_turned = sem("route_turned")
        route_copied = sem("route_copied")
        fg_w_hi = sem("fg_w_hi")
        fg_w_ready = sem("fg_w_ready")
        pick_cleared = sem("pick_cleared")
        fg_composed = sem("fg_composed")
        attn_w_hi = sem("attn_w_hi")
        attn_w_ready = sem("attn_w_ready")
        pick_copied = sem("pick_copied")
        expert_hi = sem("expert_hi")
        expert_lo = sem("expert_lo")
        xn_made = sem("xn_made")
        xn_turned = sem("xn_turned")
        xn_hi_made = sem("xn_hi_made")
        xn_lo_made = sem("xn_lo_made")
        kf_projected = sem("kf_projected")
        kf_made = sem("kf_made")
        f_made = sem("f_made")
        qg_projected = sem("qg_projected")
        qg_made = sem("qg_made")
        og_made = sem("og_made")
        sq_made = sem("sq_made")
        sq_summed = sem("sq_summed")
        rs_made = sem("rs_made")
        rs_turned = sem("rs_turned")
        rs_copied = sem("rs_copied")
        rs_spread = sem("rs_spread")
        on_made = sem("on_made")
        attn_projected = sem("attn_projected")
        attn_copied = sem("attn_copied")
        an_made = sem("an_made")
        x2n_made = sem("x2n_made")
        x2_turned = sem("x2_turned")
        x2_copied = sem("x2_copied")
        x2_lo_made = sem("x2_lo_made")
        logits_made = sem("logits_made")
        z_made = sem("z_made")
        exp_made = sem("exp_made")
        cw_made = sem("cw_made")
        cw_turned = sem("cw_turned")
        cw_hi_made = sem("cw_hi_made")
        cw_lo_made = sem("cw_lo_made")
        v_spread = sem("v_spread")
        kv_made = sem("kv_made")
        scanned = sem("scanned")
        carried = sem("carried")
        roomy_qs_made = {True: sem("pool_qs_made"), False: sem("dve_qs_made")}
        qs_made = sem("qs_made")
        qs_hi_made = sem("qs_hi_made")
        qs_lo_made = sem("qs_lo_made")
        qs_summed = sem("qs_summed")
        cw_spread = sem("cw_spread")
        xs_made = sem("xs_made")
        xs_hi_made = sem("xs_hi_made")
        xs_lo_made = sem("xs_lo_made")
        gate_done = sem("gate_done")
        up_done = sem("up_done")
        silu_done = sem("silu_done")
        h_made = sem("h_made")
        h_hi_made = sem("h_hi_made")
        h_lo_made = sem("h_lo_made")
        down_done = sem("down_done")
        tail_lo_made = sem("tail_lo_made")
        y_copied = sem("y_copied")
        y_turned = sem("y_turned")
        x_out_made = sem("x_out_made")
        x_chain = sem("x_chain")
        late_chain = sem("late_chain")
        y_chain = sem("y_chain")

        def atleast(eng, s, value):
            if not (isinstance(value, int) and value <= 0):
                eng.wait_ge(s, value)

        def ff_cols(c):
            return bass.ds((c % 2) * CHUNK, CHUNK)

        def tile_of(buf, c, i):
            return buf[:, bass.ds(c * TILES + i, 1), :].squeeze(1)

        def tiles(c):
            return bass.ds(c * TILES, TILES)

        def three(out_ap, w_hi, w_lo, v_hi, v_lo, start=True, stop=True):
            nc.tensor.matmul(out_ap, w_hi, v_hi, start=start, stop=False)
            nc.tensor.matmul(out_ap, w_hi, v_lo, start=False, stop=False)
            return nc.tensor.matmul(out_ap, w_lo, v_hi, start=False, stop=stop)

        def round_of(c, feed_forward, late, early, end):
            for slot in range(STEPS):
                n = slot + HEAD
                if n < STEPS:
                    feed_forward(n, c, late is not None)
                else:
                    feed_forward(n - STEPS, c + 1, late is not None)
                for stage in EARLY_AT.get(slot, []) if early else []:
                    early(stage, c + 2)
                for stage in LATE_AT.get(slot, []) if late else []:
                    late(stage, c + 1)
                for stage in END_AT.get(slot, []):
                    end(stage, c)

        def program(eng, feed_forward, late, early, end, expert=None, late_counted=None):
            split = 0
            for stage in EARLY:
                early(stage, 0)
                if expert and stage in SPLIT_AFTER:
                    expert(split)
                    split += 1
            for item in BESIDE.split():
                part, stage = item[0], int(item[1:] or 0)
                if part == "L":
                    late(stage, 0)
                    if late_counted and stage == LATE[-1]:
                        late_counted()
                if part == "E":
                    early(stage, 1)
                if part == "X" and expert:
                    expert(split)
                    split += 1
                if part == "F":
                    feed_forward(stage, 0, False)
            with eng.Fori(0, CHUNKS - 2) as c:
                round_of(c, feed_forward, late, early, end)
            round_of(CHUNKS - 2, feed_forward, late, None, end)
            for n in range(HEAD, STEPS):
                feed_forward(n, CHUNKS - 1, False)
            for n in range(LAG):
                feed_forward(n, CHUNKS, False)
            for stage in range(4):
                end(stage, CHUNKS - 1)

        def spread_in(c, n):
            e, j = divmod(n, NJ)
            return e if e < NE and j == (isinstance(c, int) and c == 0 and e == 0) else None

        def roomy(c):
            return isinstance(c, int) and c < 2

        def spread_bank(c, v):
            return gate_ps[0] if roomy(c) and v % 2 and (c == 0 or v < ROOMY_V) else a_ps

        def last_in_ring(n):
            if n >= H_RING:
                return n - H_RING
            return max(m for m in range(STEPS) if m % H_RING == n % H_RING) - STEPS

        def in_tail(c, n):
            return isinstance(c, int) and c == CHUNKS - 1 and n >= HEAD

        def on_pool(v):
            return v not in VECTOR_V

        def roomy_qs_count(c, v):
            mine = [u for u in range(D) if on_pool(u) == on_pool(v)]
            return len(mine) * c + mine.index(v) + 1

        def kf_banks(c):
            return (gate_ps[1], up_ps[0]) if roomy(c) else (a_ps, o_ps)

        def qg_banks(c):
            return (up_ps[1], y_ps) if roomy(c) else (a_ps, o_ps)

        block = ctx.enter_context(nc.Block())

        @block.sync
        def _(sp):
            def load_expert(n):
                landed = expert_landed[n]
                gate, up, down = ((sw_gate, sw_up, sw_down) if n == 0
                                  else (we_gate[n - 1], we_up[n - 1], we_down[n - 1]))
                s = n % STAGE
                if n >= STAGE:
                    sp.wait_ge(expert_lo, n - STAGE + 1)
                sp.dma_start(raw_gu[:, s, 0, :], gate).then_inc(landed, 16)
                sp.dma_start(raw_gu[:, s, 1, :], up).then_inc(landed, 16)
                if n == 0:
                    sp.wait_ge(stage_cleared, 1)
                whole = FD // P * P
                sp.dma_start(raw_down[:, s, 0:FD // P, :],
                             down[0:whole, :].rearrange("(j p) e -> p j e", p=P)).then_inc(landed, 16)
                sp.dma_start(raw_down[0:FD - whole, s, FD // P, :], down[whole:FD, :]).then_inc(landed, 16)

            x_tok = x[0].rearrange("(i p) e -> p i e", p=P)
            sp.dma_start(x_res[:, 0:TILES, :], x_tok[:, 0:TILES, :]).then_inc(x_in_landed[0], 16)
            for i, w in enumerate((Wq, Wk, Wv)):
                sp.dma_start(raw_qkv[:, i, :], w).then_inc(attn_w_landed, 16)
            load_expert(0)
            for c in range(1, CHUNKS):
                sp.dma_start(x_res[:, c * TILES:(c + 1) * TILES, :],
                             x_tok[:, c * TILES:(c + 1) * TILES, :]).then_inc(x_in_landed[c], 16)
            for n in range(1, NX):
                load_expert(n)
            out_tok = out[0].rearrange("(i p) e -> p i e", p=P)
            with sp.Fori(0, CHUNKS) as c:
                sp.wait_ge(x_out_made, c + 1)
                sp.dma_start(out_tok[:, tiles(c), :], x_res[:, tiles(c), :]).then_inc(out_stored, 16)
            sp.wait_ge(out_stored, 16 * CHUNKS)

        @block.gpsimd
        def _(pool):
            nc.gpsimd.memset(ident[:], 0.0)
            nc.gpsimd.memset(head_of[:], 1.0)
            nc.gpsimd.memset(head_rows[:], 1.0)
            nc.gpsimd.memset(pick_expert_f, 0.0).then_inc(pool_const, 1)
            pool.wait_ge(pool_const, 1)
            nc.gpsimd.affine_select(out=ident[:], in_=ident[:], compare_op=ALU.not_equal, fill=1.0,
                                    base=0, pattern=[[-1, P]], channel_multiplier=1)
            nc.gpsimd.affine_select(out=head_of[:], in_=head_of[:], compare_op=ALU.is_ge, fill=0.0,
                                    base=0, pattern=[[-D, HEADS]], channel_multiplier=1)
            nc.gpsimd.affine_select(out=head_rows[:], in_=head_rows[:], compare_op=ALU.is_ge, fill=0.0,
                                    base=0, pattern=[[1, P]], channel_multiplier=-D)
            nc.gpsimd.affine_select(out=pick_expert_f, in_=pick_expert_f, compare_op=ALU.not_equal,
                                    fill=1.0, base=0, pattern=[[-1, NE], [0, P]],
                                    channel_multiplier=1).then_inc(pool_const, 1)
            pool.wait_ge(pool_const, 2)
            nc.gpsimd.affine_select(out=head_of[:], in_=head_of[:], compare_op=ALU.is_ge, fill=0.0,
                                    base=D - 1, pattern=[[D, HEADS]], channel_multiplier=-1)
            nc.gpsimd.affine_select(out=head_rows[:], in_=head_rows[:], compare_op=ALU.is_ge, fill=0.0,
                                    base=D - 1, pattern=[[-1, P]], channel_multiplier=D)
            nc.gpsimd.affine_select(out=pick_expert_f, in_=pick_expert_f, compare_op=ALU.not_equal,
                                    fill=1.0, base=-LO, pattern=[[-1, NE], [0, P]],
                                    channel_multiplier=1).then_inc(consts_made, 1)
            nc.gpsimd.memset(raw_down[:], 0.0).then_inc(stage_cleared, 1)
            nc.gpsimd.memset(pick_v[:].bitcast(F32), 0.0).then_inc(pick_cleared, 1)
            nc.gpsimd.memset(cw_rows[:].bitcast(F32), 0.0).then_inc(cw_cleared, 1)
            nc.gpsimd.memset(prob[:, :, NE:2 * NE], -1.0)
            nc.gpsimd.memset(keys[:], -1.0).then_inc(keys_made, 1)

            def early(s, c):
                if 5 <= s < 5 + D:
                    v = s - 5
                    if roomy(c) and on_pool(v):
                        if v == 0:
                            pool.wait_ge(qg_made, c + 1)
                        pool.wait_ge(scanned, D * c + v + 1)
                        atleast(pool, qs_summed, D * c + v - 1)
                        nc.gpsimd.tensor_tensor(qs[:, v % 2, :], state[:, v % 2, :], q[:],
                                                ALU.mult).then_inc(roomy_qs_made[True], 1)
                    pool.wait_ge(scanned, D * c + v + 1)
                    pool.nop(nofuse=True)
                    nc.gpsimd.tensor_copy(carry[:, v:v + 1], state[:, v % 2, CHUNK - 1:CHUNK]).then_inc(carried, 1)
                    if roomy(c):
                        return
                    pool.wait_ge(qs_hi_made, D * (c - 2) + v + 1)
                    nc.gpsimd.tensor_tensor(qs_lo[:, v % 2, :], qs[:, v % 2, :], qs_hi[:, v % 2, :].bitcast(F32),
                                            ALU.subtract).then_inc(qs_lo_made, 1)

            def late(s, c):
                pass

            def end(s, c):
                pass

            def feed_forward(n, c, beside):
                if isinstance(c, int) and c == CHUNKS and n >= 1:
                    return
                if n >= 1 or not (isinstance(c, int) and c == 0):
                    before = (n - 1) % STEPS
                    if not (in_tail(c, n - 1) or in_tail(c - 1, STEPS - 1)):
                        pool.wait_ge(h_hi_made, STEPS * c + n)
                        nc.gpsimd.tensor_tensor(h_lo[:, before % H_RING, :], h[:, before % 2, :],
                                                h_hi[:, before % H_RING, :].bitcast(F32),
                                                ALU.subtract).then_inc(h_lo_made, 1)
                e = spread_in(c, n - 1)
                if e is not None and not (isinstance(c, int) and c == CHUNKS):
                    pool.wait_ge(xs_hi_made, NE * c + e + 1)
                    nc.gpsimd.tensor_tensor(xs_lo[:, e % 2, :], xs[:, e % 2, :], xs_hi[:, e % 2, :].bitcast(F32),
                                            ALU.subtract).then_inc(xs_lo_made, 1)

            def expert(n):
                pool.wait_ge(expert_hi, n + 1)
                s = n % STAGE
                nc.gpsimd.tensor_tensor(gu_lo[:, n], raw_gu[:, s], gu_hi[:, n].bitcast(F32), ALU.subtract)
                nc.gpsimd.tensor_tensor(down_lo[:, n], raw_down[:, s], down_hi[:, n].bitcast(F32),
                                        ALU.subtract).then_inc(expert_lo, 1)

            program(pool, feed_forward, late, early, end, expert)

        @block.scalar
        def _(act):
            act.dma_start(raw_fg1[:, 0, :], Wf1).then_inc(gate_w_landed, 16)
            act.dma_start(raw_fg1[:, 1, :], Wg1).then_inc(gate_w_landed, 16)
            act.dma_start(raw_fg2[:, 0, :], Wf2).then_inc(gate_w_landed, 16)
            act.dma_start(raw_fg2[:, 1, :], Wg2).then_inc(gate_w_landed, 16)
            act.dma_start(raw_route[:], gate_w).then_inc(small_w_landed, 16)
            act.dma_start(norm_w[:], norm_weight.rearrange("(p a) -> p a", a=1)).then_inc(small_w_landed, 16)
            act.dma_start(w_out[:], Wo).then_inc(small_w_landed, 16)

            def copy(dst, src):
                return nc.scalar.activation(dst, src, ACT.Copy)

            act.wait_ge(pool_const, 2)
            nc.scalar.activation(warm[:], ident[0:1, 0:1], ACT.Silu)

            def early(s, c):
                if s == 1:
                    act.wait_ge(xn_turned, c + 1)
                    atleast(act, v_spread, D * c)
                    copy(xn_hi[:], a_ps[:]).then_inc(xn_hi_made, 1)
                if s == 2:
                    act.wait_ge(kf_projected, c + 1)
                    atleast(act, scanned, D * c)
                    k_ps, f_ps = kf_banks(c)
                    nc.scalar.activation(k[:], k_ps[:], ACT.Silu)
                    nc.scalar.activation(f[:], f_ps[:], ACT.Tanh, scale=0.5).then_inc(kf_made, 1)
                if s == 3:
                    act.wait_ge(qg_projected, c + 1)
                    atleast(act, og_made, c)
                    q_ps, g_ps = qg_banks(c)
                    nc.scalar.activation(q[:], q_ps[:], ACT.Silu)
                    nc.scalar.activation(g[:], g_ps[:], ACT.Tanh, scale=0.5).then_inc(qg_made, 1)
                if 5 <= s < 5 + D and not roomy(c):
                    v = s - 5
                    act.wait_ge(qs_made, D * (c - 2) + v + 1)
                    atleast(act, qs_summed, D * c + v - 1)
                    copy(qs_hi[:, v % 2, :], qs[:, v % 2, :]).then_inc(qs_hi_made, 1)

            def late(s, c):
                if s == 14:
                    act.wait_ge(og_made, c + 1)
                    atleast(act, logits_made, c)
                    nc.scalar.activation(turns[:], og[:], ACT.Square).then_inc(sq_made, 1)
                if s == 17:
                    act.wait_ge(rs_turned, c + 1)
                    atleast(act, rs_spread, c)
                    copy(rs_rows[:], w_ps[0:HEADS, :]).then_inc(rs_copied, 1)
                if s == 19:
                    act.wait_ge(attn_projected, c + 1)
                    copy(an[:], w_tok).then_inc(attn_copied, 1)
                if s == 25:
                    act.wait_ge(x2_turned, c + 1)
                    half = ff_cols(c)
                    copy(turns[:], w_ps[:])
                    copy(ff[:, half], w_ps[:])
                    copy(ff_hi[:, half], w_ps[:]).then_inc(x2_copied, 1)
                if s == 27:
                    act.wait_ge(z_made, c + 1)
                    nc.scalar.activation(ez[:], z[:], ACT.Exp).then_inc(exp_made, 1)
                if s == 29:
                    act.wait_ge(cw_turned, c + 1)
                    if isinstance(c, int):
                        act.wait_ge(cw_cleared, 1)
                    copy(cw_rows[0:NE, ff_cols(c)], w_ps[0:NE, :]).then_inc(cw_hi_made, 1)

            def feed_forward(n, c, beside):
                if not (isinstance(c, int) and c == CHUNKS):
                    act.wait_ge(gate_done, STEPS * c + n + 1)
                    atleast(act, h_made, STEPS * c + max(n - 1, 0))
                    r = ROWS[n % NJ][1]
                    nc.scalar.activation(sg[0:r, n % 2, :], gate_ps[n % 2][0:r, :], ACT.Silu).then_inc(silu_done, 1)
                elif n >= 1:
                    return
                if n >= 1 or not (isinstance(c, int) and c == 0):
                    before = (n - 1) % STEPS
                    act.wait_ge(h_made, STEPS * c + n)
                    atleast(act, down_done, STEPS * c + n - 1 - before + last_in_ring(before) + 1)
                    copy(h_hi[:, before % H_RING, :], h[:, before % 2, :]).then_inc(h_hi_made, 1)
                e = spread_in(c, n - 1)
                if e is not None:
                    act.wait_ge(xs_made, NE * c + e + 1)
                    atleast(act, up_done, STEPS * c + (NJ * e if e >= 2 else 0))
                    copy(xs_hi[:, e % 2, :], xs[:, e % 2, :]).then_inc(xs_hi_made, 1)

            def end(s, c):
                if s == 0:
                    act.wait_ge(down_done, STEPS * (c + 1))
                    copy(y_t[:], y_ps[:]).then_inc(y_copied, 1)

            def expert(n):
                act.wait_ge(expert_landed[n], 64)
                if n == 0:
                    act.wait_ge(stage_cleared, 1)
                s = n % STAGE
                copy(gu_hi[:, n], raw_gu[:, s])
                copy(down_hi[:, n], raw_down[:, s]).then_inc(expert_hi, 1)

            act.wait_ge(attn_w_landed, 48)
            copy(proj_hi[:, 0:2, :], raw_qkv[:, 0:2, :]).then_inc(attn_w_hi, 1)
            copy(vrep_hi[:].rearrange("p v (h k) -> p v h k", k=D),
                 raw_qkv[:, 2, :].rearrange("p (h v) -> p v h", v=D).unsqueeze(3).to_broadcast([P, D, HEADS, D])
                 ).then_inc(attn_w_hi, 1)
            program(act, feed_forward, late, early, end, expert)

        @block.vector
        def _(dve):
            v_cols = raw_qkv[:, 2, :].rearrange("p (h v) -> p v h", v=D).unsqueeze(3).to_broadcast([P, D, HEADS, D])
            vh = vrep_hi[:].rearrange("p v (h k) -> p v h k", k=D)
            vl = vrep_lo[:].rearrange("p v (h k) -> p v h k", k=D)

            Y_LINKS = 3 + 1 + 3 * NEWTON_STEPS + 1
            per_chunk = {y_chain: Y_LINKS}
            done = {}

            def link(chain, c, ins):
                done[chain] = done.get(chain, 0) + 1
                ins.then_inc(chain, 1)
                dve.wait_ge(chain, c * per_chunk.get(chain, 0) + done[chain])

            def rsqrt(chain, c, out_ap, n, steps=range(NEWTON_STEPS)):
                v, y, t, mh = var_eps[:, 0:n], out_ap, newton[:, 0:n], minus_half[:, 0:n]
                if 0 in steps:
                    nc.vector.tensor_scalar(mh, v, -0.5, None, ALU.mult)
                    link(chain, c, nc.vector.tensor_scalar(y.bitcast(I32), v.bitcast(I32), -0.5,
                                                           float(RSQRT_MAGIC), ALU.mult, ALU.add))
                for step in steps:
                    link(chain, c, nc.vector.tensor_tensor(t, y, y, ALU.mult))
                    link(chain, c, nc.vector.tensor_tensor(t, t, mh, ALU.mult))
                    last = nc.vector.scalar_tensor_tensor(y, t, 1.5, y, ALU.add, ALU.mult)
                    if step < steps[-1]:
                        link(chain, c, last)
                return last

            def tile_stats(chain, c, src, mom, count=TILES):
                for i in range(count):
                    last = nc.vector.bn_stats(stats[:, i, :], src(i))
                link(chain, c, last)
                dve.nop(nofuse=True)
                for i in range(count):
                    last = nc.vector.bn_aggr(mom[:, i, :], stats[:, i, :])
                link(chain, c, last)

            def add_eps(chain, c, mom, count=TILES):
                link(chain, c, nc.vector.tensor_scalar(var_eps[:, 0:count], mom[:, 0:count, 1], EPS, None,
                                                       ALU.add))

            def normalise(dst, src, mean, rstd):
                for i in range(TILES):
                    last = nc.vector.tensor_scalar(dst[:, i, :], src(i), mean(i), rstd(i),
                                                   ALU.subtract, ALU.mult)
                return last

            def mean(i):
                return moments[:, i, 0:1]

            def rstd(i):
                return rs[:, i:i + 1]

            def spread(ap):
                return ap.unsqueeze(2).to_broadcast([P, TILES, NE])

            def x_rsqrt(c, count):
                at, count = c * TILES, count * TILES
                add_eps(x_chain, 0, x_mom[:, at:at + count, :], count)
                link(x_chain, 0, rsqrt(x_chain, 0, x_rs[:, at:at + count], count))

            def key_value(c, v):
                dve.wait_ge(v_spread, D * c + v + 1)
                kv = spread_bank(c, v)
                nc.vector.tensor_tensor(kv[:], kv[:], k[:], ALU.mult).then_inc(kv_made, 1)

            def early(s, c):
                if s == 0:
                    if isinstance(c, int) and c == 0:
                        dve.wait_ge(x_in_landed[0], 16)
                        tile_stats(x_chain, 0, lambda i: x_res[:, i, :], x_mom)
                        x_rsqrt(0, 1)
                    atleast(dve, xn_turned, c)
                    normalise(xn, lambda i: tile_of(x_res, c, i),
                              lambda i: x_mom[:, bass.ds(c * TILES + i, 1), 0:1].squeeze(1),
                              lambda i: x_rs[:, bass.ds(c * TILES + i, 1)]).then_inc(xn_made, 1)
                    if isinstance(c, int) and c == 0:
                        qk_weights()
                if s == 1:
                    dve.wait_ge(xn_hi_made, c + 1)
                    nc.vector.tensor_tensor(xn_lo[:], a_ps[:], xn_hi[:].bitcast(F32),
                                            ALU.subtract).then_inc(xn_lo_made, 1)
                    if isinstance(c, int) and c == 0:
                        fg_weights()
                        v_weights()
                        selectors()
                if 4 <= s < 4 + D:
                    v = s - 4
                    if v == 0:
                        dve.wait_ge(kf_made, c + 1)
                        nc.vector.tensor_scalar(f[:], f[:], 0.5, 0.5, ALU.mult, ALU.add).then_inc(f_made, 1)
                    if v == 0 or spread_bank(c, v) is spread_bank(c, v - 1):
                        key_value(c, v)
                    if v == 0:
                        dve.wait_ge(f_made, c + 1)
                    dve.wait_ge(kv_made, D * c + v + 1)
                    kv = spread_bank(c, v)
                    atleast(dve, carried, D * c + v - 1)
                    first_state = 0.0 if isinstance(c, int) and c == 0 else carry[:, v:v + 1]
                    nc.vector.tensor_tensor_scan(state[:, v % 2, :], f[:], kv[:], first_state,
                                                 ALU.mult, ALU.add).then_inc(scanned, 1)
                    if v + 1 < D and spread_bank(c, v + 1) is not spread_bank(c, v):
                        key_value(c, v + 1)
                    if isinstance(c, int) and c == 0 and v < D - 2:
                        per_v = (CHUNKS - 1) * TILES // (D - 2)
                        for i in range(TILES + per_v * v, TILES + per_v * (v + 1)):
                            if i % TILES == 0:
                                dve.wait_ge(x_in_landed[i // TILES], 16)
                            last = nc.vector.bn_stats(stats[:, i, :], x_res[:, i, :])
                        if v == D - 3:
                            link(x_chain, 0, last)
                    if roomy(c) and on_pool(v):
                        return
                    if v == (VECTOR_V[0] if roomy(c) else 0):
                        dve.wait_ge(qg_made, c + 1)
                    dve.wait_ge(scanned, D * c + v + 1)
                    if roomy(c):
                        atleast(dve, qs_summed, D * c + v - 1)
                    elif v >= 2:
                        dve.wait_ge(qs_lo_made, D * (c - 2) + v - 1)
                    made = roomy_qs_made[False] if roomy(c) else qs_made
                    nc.vector.tensor_tensor(qs[:, v % 2, :], state[:, v % 2, :], q[:], ALU.mult).then_inc(made, 1)
                if s == 12 and isinstance(c, int) and c == 0:
                    for i in range(TILES, CHUNKS * TILES):
                        last = nc.vector.bn_aggr(x_mom[:, i, :], stats[:, i, :])
                    link(x_chain, 0, last)
                if s == 13:
                    dve.wait_ge(qs_summed, D * c + D)
                    nc.vector.scalar_tensor_tensor(og[:], g[:], 1.0, o_ps[:], ALU.add,
                                                   ALU.mult).then_inc(og_made, 1)
                    if isinstance(c, int) and c == 0:
                        x_rsqrt(1, CHUNKS - 1)

            def late(s, c):
                def lk(ins):
                    link(late_chain, c, ins)

                if s == 15:
                    dve.wait_ge(sq_summed, c + 1)
                    done[late_chain] = 0
                    lk(nc.vector.tensor_scalar(var_eps[:], w_ps[:, 0:TILES * HEADS], (SCALE / 2) ** 2 / D, EPS,
                                               ALU.mult, ALU.add))
                    lk(rsqrt(late_chain, c, rs[:], TILES * HEADS, range(0, 1)))
                if s == 16:
                    rsqrt(late_chain, c, rs[:], TILES * HEADS, range(1, NEWTON_STEPS)).then_inc(rs_made, 1)
                if s == 18:
                    dve.wait_ge(rs_spread, c + 1)
                    nc.vector.scalar_tensor_tensor(turns[:], og[:], norm_half[:], w_ps[:], ALU.mult,
                                                   ALU.mult).then_inc(on_made, 1)
                if s == 19:
                    dve.wait_ge(attn_copied, c + 1)
                    tile_stats(late_chain, c, lambda i: an[:, i, :], moments)
                    add_eps(late_chain, c, moments)
                if s == 20:
                    lk(rsqrt(late_chain, c, rs[:, 0:TILES], TILES))
                if s == 21:
                    normalise(an, lambda i: an[:, i, :], mean, rstd).then_inc(an_made, 1)
                    dve.wait_ge(an_made, c + 1)
                    lk(nc.vector.tensor_tensor(x_res[:, tiles(c), :], an[:], x_res[:, tiles(c), :],
                                               ALU.add))
                if s == 22:
                    tile_stats(late_chain, c, lambda i: tile_of(x_res, c, i), moments)
                    add_eps(late_chain, c, moments)
                if s == 23:
                    lk(rsqrt(late_chain, c, rs[:, 0:TILES], TILES))
                if s == 24:
                    normalise(an, lambda i: tile_of(x_res, c, i), mean, rstd).then_inc(x2n_made, 1)
                if s == 25:
                    dve.wait_ge(x2_copied, c + 1)
                    half = ff_cols(c)
                    nc.vector.tensor_tensor(ff_lo[:, half], w_ps[:], ff_hi[:, half].bitcast(F32),
                                            ALU.subtract).then_inc(x2_lo_made, 1)
                if s == 26:
                    dve.wait_ge(logits_made, c + 1)
                    logits = w_ps[:, 0:TILES * NE].rearrange("p (i e) -> p i e", e=NE)
                    lk(nc.vector.tensor_reduce(top[:, 0, :], logits, AX_X, ALU.max))
                    nc.vector.tensor_tensor(z[:], logits, spread(top[:, 0, :]), ALU.subtract).then_inc(z_made, 1)
                if s == 27:
                    dve.wait_ge(exp_made, c + 1)
                    lk(nc.vector.tensor_reduce(top[:, 1, :], ez[:], AX_X, ALU.add))
                    lk(nc.vector.reciprocal(top[:, 2, :], top[:, 1, :]))
                    lk(nc.vector.tensor_tensor(prob[:, :, 0:NE], ez[:], spread(top[:, 2, :]), ALU.mult))
                    dve.nop(nofuse=True)
                    for i in range(TILES):
                        last = nc.vector.max(best[:, i, :], prob[:, i, 0:NE])
                    lk(last)
                    nc.vector.tensor_copy(keys[:, :, 0:2], best[:, :, 0:2])
                    lk(nc.vector.tensor_tensor(top[:, 3, :], best[:, :, 0], best[:, :, 1], ALU.add))
                if s == 28:
                    dve.nop(nofuse=True)
                    for i in range(TILES):
                        nc.vector.match_replace(rest[:, i, :], keys[:, i, :], prob[:, i, :], 0.0)
                    lk(nc.vector.tensor_scalar(top[:, 4, :], top[:, 3, :], 1e-20, None, ALU.add))
                    nc.vector.tensor_tensor(cand[:], prob[:, :, 0:NE], rest[:, :, 0:NE], ALU.subtract)
                    lk(nc.vector.reciprocal(top[:, 5, :], top[:, 4, :]))
                    nc.vector.tensor_tensor(cw[:], cand[:], spread(top[:, 5, :]), ALU.mult).then_inc(cw_made, 1)
                if s == 29:
                    dve.wait_ge(cw_hi_made, c + 1)
                    nc.vector.tensor_tensor(cw_rows[LO:LO + NE, ff_cols(c)], w_ps[0:NE, :],
                                            cw_rows[0:NE, ff_cols(c)].bitcast(F32),
                                            ALU.subtract).then_inc(cw_lo_made, 1)

            def tail_lo(n, c):
                if in_tail(c, n):
                    dve.wait_ge(h_hi_made, STEPS * c + n + 1)
                    nc.vector.tensor_tensor(h_lo[:, n % H_RING, :], h[:, n % 2, :], h_hi[:, n % H_RING, :].bitcast(F32),
                                            ALU.subtract).then_inc(tail_lo_made, 1)

            def feed_forward(n, c, beside):
                if isinstance(c, int) and c == CHUNKS:
                    if n == 0:
                        tail_lo(STEPS - 1, c - 1)
                    return
                r = ROWS[n % NJ][1]
                dve.wait_ge(silu_done, STEPS * c + n + 1)
                dve.wait_ge(up_done, STEPS * c + n + 1)
                if in_tail(c, n - 2):
                    dve.wait_ge(tail_lo_made, n - 2 - HEAD + 1)
                else:
                    atleast(dve, h_lo_made, STEPS * c + max(n - 1, 0))
                nc.vector.tensor_tensor(h[0:r, n % 2, :], sg[0:r, n % 2, :], up_ps[n % 2][0:r, :],
                                        ALU.mult).then_inc(h_made, 1)
                e = spread_in(c, n)
                if e is not None:
                    dve.wait_ge(cw_spread, NE * c + e + 1)
                    atleast(dve, xs_lo_made, NE * c + e - 1)
                    nc.vector.tensor_tensor(xs[:, e % 2, :], ff[:, ff_cols(c)], w_ps[:],
                                            ALU.mult).then_inc(xs_made, 1)
                tail_lo(n - 1, c)

            def end(s, c):
                if s == 1:
                    dve.wait_ge(y_turned, c + 1)
                    done[y_chain] = 0
                    tile_stats(y_chain, c, lambda i: a_tok[:, i, :], moments)
                    add_eps(y_chain, c, moments)
                if s == 2:
                    link(y_chain, c, rsqrt(y_chain, c, rs[:, 0:TILES], TILES))
                if s == 3:
                    link(y_chain, c, normalise(an, lambda i: a_tok[:, i, :], mean, rstd))
                    nc.vector.tensor_tensor(x_res[:, tiles(c), :], an[:], x_res[:, tiles(c), :],
                                            ALU.add).then_inc(x_out_made, 1)

            def late_counted():
                per_chunk[late_chain] = done[late_chain]

            def qk_weights():
                dve.wait_ge(attn_w_hi, 1)
                nc.vector.tensor_tensor(proj_lo[:, 0:2, :], raw_qkv[:, 0:2, :], proj_hi[:, 0:2, :].bitcast(F32),
                                        ALU.subtract).then_inc(attn_w_ready, 1)
                dve.wait_ge(fg1_turned, 1)
                nc.vector.tensor_copy(fg1_t[:], y_ps[0:D, 0:2 * E].rearrange("d (g e) -> d g e", g=2)
                                      ).then_inc(fg1_copied, 1)

            def fg_weights():
                dve.wait_ge(fg_composed, 1)
                fg = o_ps[:, 0:2 * E].rearrange("p (g e) -> p g e", g=2)
                nc.vector.tensor_copy(proj_hi[:, 2:4, :], fg).then_inc(fg_w_hi, 1)
                dve.wait_ge(fg_w_hi, 1)
                nc.vector.tensor_tensor(proj_lo[:, 2:4, :], fg, proj_hi[:, 2:4, :].bitcast(F32),
                                        ALU.subtract).then_inc(fg_w_ready, 1)

            def v_weights():
                dve.wait_ge(attn_w_hi, 2)
                nc.vector.tensor_tensor(vl, v_cols, vh.bitcast(F32), ALU.subtract).then_inc(attn_w_ready, 1)

            def selectors():
                dve.wait_ge(route_turned, 1)
                nc.vector.tensor_copy(route_t[:], y_ps[:, 2 * E:2 * E + NE])
                nc.vector.tensor_scalar(norm_half[:], norm_w[:], SCALE / 2, None, ALU.mult).then_inc(route_copied, 1)
                dve.wait_ge(consts_made, 1)
                dve.wait_ge(pick_cleared, 1)
                nc.vector.tensor_copy(pick_v[:, D - 1:].rearrange("p (h w) -> p h w", w=D)[:, :, 0], head_of[:])
                nc.vector.tensor_copy(pick_expert[:], pick_expert_f).then_inc(pick_copied, 1)
                dve.wait_ge(route_copied, 1)
                dve.wait_ge(keys_made, 1)

            program(dve, feed_forward, late, early, end, None, late_counted)

        @block.tensor
        def _(pe):
            def turn(dst, src, rows=P):
                return nc.tensor.transpose(dst, src, ident[0:rows, 0:rows])

            def small_weights():
                pe.wait_ge(gate_w_landed, 16 * 4)
                for i in range(2):
                    last = turn(y_ps[0:D, i * E:(i + 1) * E], raw_fg1[:, i, :])
                last.then_inc(fg1_turned, 1)
                pe.wait_ge(fg1_copied, 1)
                for i in range(2):
                    last = nc.tensor.matmul(o_ps[:, i * E:(i + 1) * E], fg1_t[:, i, :], raw_fg2[:, i, :],
                                            start=True, stop=True)
                last.then_inc(fg_composed, 1)
                pe.wait_ge(small_w_landed, 16 * 3)
                turn(y_ps[:, 2 * E:2 * E + NE], raw_route[:], NE).then_inc(route_turned, 1)

            def spread_v(v, c):
                if v == 0 and not roomy(c):
                    pe.wait_ge(qg_made, c + 1)
                if v == 0 and isinstance(c, int):
                    pe.wait_ge(attn_w_ready, 2)
                before = [u for u in range(v) if spread_bank(c, u) is spread_bank(c, v)]
                atleast(pe, scanned, D * c + (before[-1] + 1 if before else 0))
                three(spread_bank(c, v)[:], vrep_hi[:, v, :], vrep_lo[:, v, :], xn_hi[:],
                      xn_lo[:]).then_inc(v_spread, 1)

            def early(s, c):
                if s == 1:
                    if isinstance(c, int) and c == 0:
                        pe.wait_ge(consts_made, 1)
                    pe.wait_ge(xn_made, c + 1)
                    atleast(pe, scanned, D * c)
                    for i in range(TILES):
                        last = turn(a_tok[:, i, :], xn[:, i, :])
                    last.then_inc(xn_turned, 1)
                    if isinstance(c, int) and c == 0:
                        small_weights()
                if s == 2:
                    pe.wait_ge(xn_lo_made, c + 1)
                    if isinstance(c, int):
                        pe.wait_ge(attn_w_ready, 1)
                    k_ps, f_ps = kf_banks(c)
                    if roomy(c):
                        atleast(pe, kf_made, c)
                    three(k_ps[:], proj_hi[:, 1, :], proj_lo[:, 1, :], xn_hi[:], xn_lo[:])
                    if isinstance(c, int):
                        pe.wait_ge(fg_w_ready, 1)
                    atleast(pe, og_made, c)
                    three(f_ps[:], proj_hi[:, 2, :], proj_lo[:, 2, :], xn_hi[:], xn_lo[:]).then_inc(kf_projected, 1)
                if s == 3:
                    if roomy(c):
                        atleast(pe, qg_made, c)
                    else:
                        pe.wait_ge(kf_made, c + 1)
                    if roomy(c):
                        spread_v(0, c)
                    q_ps, g_ps = qg_banks(c)
                    three(q_ps[:], proj_hi[:, 0, :], proj_lo[:, 0, :], xn_hi[:], xn_lo[:])
                    if isinstance(c, int) and c == 0:
                        pe.wait_ge(route_copied, 1)
                    three(g_ps[:], proj_hi[:, 3, :], proj_lo[:, 3, :], xn_hi[:], xn_lo[:]).then_inc(qg_projected, 1)
                if 4 <= s < 4 + D and not (roomy(c) and s == 4):
                    spread_v(s - 4, c)
                if 6 <= s < 6 + D:
                    v = s - 6
                    pick = pick_v[:, D - 1 - v:D - 1 - v + E]
                    if v == 0 and isinstance(c, int):
                        pe.wait_ge(pick_copied, 1)
                    if roomy(c):
                        pe.wait_ge(roomy_qs_made[on_pool(v)], roomy_qs_count(c, v))
                        nc.tensor.matmul(o_ps[:], pick.bitcast(F32), qs[:, v % 2, :], start=(v == 0),
                                         stop=(v == D - 1)).then_inc(qs_summed, 1)
                        return
                    pe.wait_ge(qs_lo_made, D * (c - 2) + v + 1)
                    nc.tensor.matmul(o_ps[:], pick, qs_hi[:, v % 2, :], start=(v == 0), stop=False)
                    nc.tensor.matmul(o_ps[:], pick, qs_lo[:, v % 2, :], start=False,
                                     stop=(v == D - 1)).then_inc(qs_summed, 1)

            def late(s, c):
                def xs_read():
                    if not (isinstance(c, int) and c == 0):
                        pe.wait_ge(xs_made, NE * (c - 1) + min(LATE_STEP[s] // NJ + 1, NE))

                if s == 15:
                    pe.wait_ge(sq_made, c + 1)
                    xs_read()
                    for i in range(TILES):
                        last = nc.tensor.matmul(w_ps[:, i * HEADS:(i + 1) * HEADS], turns[:, i * P:(i + 1) * P],
                                                head_of[:], start=True, stop=True)
                    last.then_inc(sq_summed, 1)
                if s == 17:
                    pe.wait_ge(rs_made, c + 1)
                    xs_read()
                    for i in range(TILES):
                        last = turn(w_ps[0:HEADS, i * P:(i + 1) * P], rs[:, i * HEADS:(i + 1) * HEADS])
                    last.then_inc(rs_turned, 1)
                if s == 18:
                    pe.wait_ge(rs_copied, c + 1)
                    xs_read()
                    nc.tensor.matmul(w_ps[:], head_rows[:], rs_rows[:], start=True, stop=True).then_inc(rs_spread, 1)
                if s == 19:
                    pe.wait_ge(on_made, c + 1)
                    xs_read()
                    for i in range(TILES):
                        last = nc.tensor.matmul(w_tok[:, i, :], turns[:, i * P:(i + 1) * P], w_out[:],
                                                start=True, stop=True)
                    last.then_inc(attn_projected, 1)
                if s == 25:
                    pe.wait_ge(x2n_made, c + 1)
                    xs_read()
                    for i in range(TILES):
                        last = turn(w_tok[:, i, :], an[:, i, :])
                    last.then_inc(x2_turned, 1)
                if s == 26:
                    pe.wait_ge(x2_lo_made, c + 1)
                    xs_read()
                    for i in range(TILES):
                        last = nc.tensor.matmul(w_ps[:, i * NE:(i + 1) * NE], turns[:, i * P:(i + 1) * P],
                                                route_t[:], start=True, stop=True)
                    last.then_inc(logits_made, 1)
                if s == 29:
                    pe.wait_ge(cw_made, c + 1)
                    xs_read()
                    for i in range(TILES):
                        last = turn(w_ps[0:NE, i * P:(i + 1) * P], cw[:, i, :])
                    last.then_inc(cw_turned, 1)

            def down(n, c):
                r = ROWS[n % NJ][1]
                e, j = divmod(n, NJ)
                if in_tail(c, n):
                    pe.wait_ge(tail_lo_made, n - HEAD + 1)
                else:
                    pe.wait_ge(h_lo_made, STEPS * c + n + 1)
                if n == 0:
                    atleast(pe, y_copied, c)
                three(y_ps[:], down_hi[0:r, e, j, :], down_lo[0:r, e, j, :], h_hi[0:r, n % H_RING, :],
                      h_lo[0:r, n % H_RING, :], start=(n == 0), stop=(n == STEPS - 1)).then_inc(down_done, 1)

            left_by = {15: rs_made, 17: rs_copied, 18: on_made, 19: attn_copied, 25: x2_lo_made,
                       26: z_made, 29: cw_lo_made}

            def bank_left(e):
                stages = [stage for stage in left_by if LATE_STEP[stage] < NJ * e]
                return left_by[stages[-1]] if stages else None

            def feed_forward(n, c, beside):
                if isinstance(c, int) and c == CHUNKS:
                    down(STEPS - LAG + n, c - 1)
                    return
                e, j = divmod(n, NJ)
                row, r = ROWS[j]
                half = ff_cols(c)
                x_hi, x_lo = ff_hi[:, half], ff_lo[:, half]
                if n == 0 and isinstance(c, int) and c == 0:
                    pe.wait_ge(qg_made, 2)
                    pe.wait_ge(scanned, D + ROOMY_V)
                if n == 0:
                    pe.wait_ge(x2_lo_made, c + 1)
                if j == 0 and isinstance(c, int) and c == 0 or n >= HEAD and j == 0:
                    pe.wait_ge(expert_lo, e + 1)
                atleast(pe, silu_done, STEPS * c + max(n - 1, 0))
                three(gate_ps[n % 2][0:r, :], gu_hi[:, e, 0, row:row + r], gu_lo[:, e, 0, row:row + r],
                      x_hi, x_lo).then_inc(gate_done, 1)
                if e >= 1:
                    pe.wait_ge(xs_lo_made, NE * c + e)
                    u_hi, u_lo = xs_hi[:, (e - 1) % 2, :], xs_lo[:, (e - 1) % 2, :]
                else:
                    u_hi, u_lo = x_hi, x_lo
                atleast(pe, h_made, STEPS * c + max(n - 1, 0))
                three(up_ps[n % 2][0:r, :], gu_hi[:, e, 1, row:row + r], gu_lo[:, e, 1, row:row + r],
                      u_hi, u_lo).then_inc(up_done, 1)
                if spread_in(c, n) is not None:
                    if e == 0:
                        pe.wait_ge(cw_lo_made, c + 1)
                    if e >= 1:
                        pe.wait_ge(xs_made, NE * c + e)
                    if beside and bank_left(e):
                        pe.wait_ge(bank_left(e), c + 2)
                    pe.nop(nofuse=True)
                    nc.tensor.matmul(w_ps[:], pick_expert[:, e, :], cw_rows[:, half],
                                     start=True, stop=True).then_inc(cw_spread, 1)
                if n >= LAG:
                    down(n - LAG, c)
                elif not (isinstance(c, int) and c == 0):
                    down(STEPS - LAG + n, c - 1)

            def end(s, c):
                if s == 1:
                    pe.wait_ge(y_copied, c + 1)
                    pe.wait_ge(scanned, D * min(c + 3, CHUNKS) if isinstance(c, int) else D * (c + 3))
                    for i in range(TILES):
                        last = turn(a_tok[:, i, :], y_t[:, i * P:(i + 1) * P])
                    last.then_inc(y_turned, 1)

            program(pe, feed_forward, late, early, end)


_INS = ["x", "Wq", "Wk", "Wv", "Wo", "Wf1", "Wf2", "Wg1", "Wg2", "norm_weight"]
_FFN = ["gate_w", "we_gate", "we_up", "we_down", "sw_gate", "sw_up", "sw_down"]


def kernel(**inputs):
    import numpy as np
    import concourse.bacc as bacc
    from concourse.bass_utils import run_bass_kernel_spmd

    nc = bacc.Bacc("TRN2", target_bir_lowering=False, num_devices=1)
    arrays, args = {}, []
    for name in ["L0_attn_" + n for n in _INS] + ["L0_ffn_" + n for n in _FFN]:
        a = np.ascontiguousarray(inputs[name])
        arrays[f"in_{name}"] = a
        args.append(nc.dram_tensor(f"in_{name}", a.shape, mybir.dt.from_np(a.dtype), kind="ExternalInput").ap())
    shape = inputs["L0_attn_x"].shape
    out = nc.dram_tensor("out_0", shape, F32, kind="ExternalOutput").ap()
    build(nc, *args, out)
    r = run_bass_kernel_spmd(nc, [arrays], core_ids=[0])
    return r.results[0]["out_0"]
```
